# Optimizing a Trainium2 kernel written in Bass

```python
import numpy as np
import jax
import jax.numpy as jnp

def _softmax(x, axis=-1):
    return jax.nn.softmax(x, axis=axis)

def _gelu(x):
    return jax.nn.gelu(x, approximate=True)

def _silu(x):
    return jax.nn.silu(x)

def _sigmoid(x):
    return jax.nn.sigmoid(x)

def _layernorm(x, axis=-1, eps=1e-05):
    m = jnp.mean(x, axis=axis, keepdims=True)
    v = jnp.var(x, axis=axis, keepdims=True)
    return (x - m) / jnp.sqrt(v + eps)

def _scatter_add(tgt, idx, src, axis=0):
    return tgt.at[idx].add(src)

def _segment_sum(src, seg, n):
    return jax.ops.segment_sum(src, seg, n)
kernel_name = 'mk_adj_preln_d4_adj_r2_0e9ae0'

def setup_inputs(seed: int=0):
    np.random.seed(seed)
    _w = jnp.asarray

    def _rec_inputs():
        import jax
        import jax.numpy as jnp
        _gk = jax.random.key(seed)
        x = -0.0002928 + 1 * jax.random.normal(jax.random.fold_in(_gk, 1), (128, 128, 128), jnp.float32)
        _a = jax.random.bernoulli(jax.random.fold_in(_gk, 2), 0.0625, (128, 128, 128))
        _a = jnp.logical_or(_a, jnp.swapaxes(_a, -1, -2))
        _a = jnp.logical_or(_a, jnp.eye(128, dtype=bool))
        _af = _a.astype(jnp.float32)
        _af = _af * jax.random.uniform(jax.random.fold_in(_gk, 3), (128, 128, 128), jnp.float32, 0.05, 1)
        adj = _af
        _nm = jnp.ones((128, 128), dtype=bool)
        nodemask = jnp.where(_nm, 1.0, 0.0).astype(jnp.int32)
        return (x, adj, nodemask)
    x, adj, nodemask = _rec_inputs()

    def _L0_gnn_setup():
        import jax, jax.numpy as jnp
        import numpy as np
        HIDDEN = 128
        NEG_INF = -1e+30
        key = jax.random.key(seed)
        k1, k2, k3, k4 = jax.random.split(key, 4)
        B, S, H = (4, 2048, HIDDEN)
        matrix = jax.random.normal(k1, (B, S, H), dtype=jnp.float32)
        mask = jax.random.randint(k2, (B, S), 0, 2, dtype=jnp.int32)
        adj = jax.random.uniform(k3, (B, S, S), dtype=jnp.float32)
        limit = float(np.sqrt(6.0 / (H + H)))
        W = jax.random.uniform(k4, (H, H), dtype=jnp.float32, minval=-limit, maxval=limit)
        return {'matrix': matrix, 'mask': mask, 'adj': adj, 'W': W}
    _L0_gnn_all = _L0_gnn_setup()
    _L0_gnn_in = {k: v for k, v in _L0_gnn_all.items() if k in ('W',)}
    del _L0_gnn_all

    def _L1_gnn_setup():
        import jax, jax.numpy as jnp
        import numpy as np
        B, N, IN_DIM, OUT_DIM, H = (4, 1024, 128, 128, 8)
        ATN = OUT_DIM // H
        key = jax.random.key(seed)
        k1, k2, k3, k4, k5 = jax.random.split(key, 5)
        x = jax.random.normal(k1, (B, N, IN_DIM), dtype=jnp.float32)
        adj = jax.random.uniform(k2, (B, N, N), dtype=jnp.float32)
        W = jax.random.normal(k3, (H, IN_DIM, ATN), dtype=jnp.float32) / np.sqrt(IN_DIM)
        b = jax.random.normal(k4, (H, ATN), dtype=jnp.float32) * 0.01
        C = jax.random.normal(k5, (H, ATN, ATN), dtype=jnp.float32) / np.sqrt(ATN)
        return {'x': x, 'adj': adj, 'W': W, 'b': b, 'C': C}
    _L1_gnn_all = _L1_gnn_setup()
    _L1_gnn_in = {k: v for k, v in _L1_gnn_all.items() if k in ('W', 'b', 'C')}
    del _L1_gnn_all

    def _L2_gnn_setup():
        import jax, jax.numpy as jnp
        import numpy as np
        B, N, D, C, L = (64, 256, 128, 128, 5)
        EDGE_P = 0.02

        def _gru_cell(m, h, w_ih, w_hh, b_ih, b_hh):
            gi = m @ w_ih.T + b_ih
            gh = h @ w_hh.T + b_hh
            i_r, i_z, i_n = jnp.split(gi, 3, axis=-1)
            h_r, h_z, h_n = jnp.split(gh, 3, axis=-1)
            r = jax.nn.sigmoid(i_r + h_r)
            z = jax.nn.sigmoid(i_z + h_z)
            n = jnp.tanh(i_n + r * h_n)
            return (1.0 - z) * n + z * h
        key = jax.random.key(seed)
        ks = jax.random.split(key, 8)
        x = jax.random.normal(ks[0], (B, N, D), dtype=jnp.float32)
        adj = (jax.random.uniform(ks[1], (B, N, N)) < EDGE_P).astype(jnp.float32)
        mask = jnp.ones((B, N), dtype=jnp.float32)
        s = 1.0 / np.sqrt(C).astype(np.float32)
        weight = jax.random.uniform(ks[2], (L, C, C), minval=-s, maxval=s, dtype=jnp.float32)
        w_ih = jax.random.uniform(ks[3], (3 * C, C), minval=-s, maxval=s, dtype=jnp.float32)
        w_hh = jax.random.uniform(ks[4], (3 * C, C), minval=-s, maxval=s, dtype=jnp.float32)
        b_ih = jax.random.uniform(ks[5], (3 * C,), minval=-s, maxval=s, dtype=jnp.float32)
        b_hh = jax.random.uniform(ks[6], (3 * C,), minval=-s, maxval=s, dtype=jnp.float32)
        return dict(x=x, adj=adj, mask=mask, weight=weight, w_ih=w_ih, w_hh=w_hh, b_ih=b_ih, b_hh=b_hh)
    _L2_gnn_all = _L2_gnn_setup()
    _L2_gnn_in = {k: v for k, v in _L2_gnn_all.items() if k in ('weight', 'w_ih', 'w_hh', 'b_ih', 'b_hh')}
    del _L2_gnn_all

    def _L3_gnn_setup():
        import jax, jax.numpy as jnp
        import numpy as np
        key = jax.random.key(seed)
        k1, k2, k3, k4 = jax.random.split(key, 4)
        B, N, F_in, F_out = (8, 1024, 128, 128)
        x = jax.random.normal(k1, (B, N, F_in), dtype=jnp.float32)
        adj = jax.random.uniform(k2, (B, N, N), dtype=jnp.float32)
        stdv = 1.0 / np.sqrt(F_out)
        weight = jax.random.uniform(k3, (F_in, F_out), dtype=jnp.float32, minval=-stdv, maxval=stdv)
        bias = jax.random.uniform(k4, (F_out,), dtype=jnp.float32, minval=-stdv, maxval=stdv)
        return {'x': x, 'adj': adj, 'weight': weight, 'bias': bias}
    _L3_gnn_all = _L3_gnn_setup()
    _L3_gnn_in = {k: v for k, v in _L3_gnn_all.items() if k in ('weight', 'bias')}
    del _L3_gnn_all
    return {'x': x, 'adj': adj, 'nodemask': nodemask, 'L0_gnn_W': _L0_gnn_in['W'], 'L1_gnn_W': _L1_gnn_in['W'], 'L1_gnn_b': _L1_gnn_in['b'], 'L1_gnn_C': _L1_gnn_in['C'], 'L2_gnn_weight': _L2_gnn_in['weight'], 'L2_gnn_w_ih': _L2_gnn_in['w_ih'], 'L2_gnn_w_hh': _L2_gnn_in['w_hh'], 'L2_gnn_b_ih': _L2_gnn_in['b_ih'], 'L2_gnn_b_hh': _L2_gnn_in['b_hh'], 'L3_gnn_weight': _L3_gnn_in['weight'], 'L3_gnn_bias': _L3_gnn_in['bias']}

def reference(x, adj, nodemask, L0_gnn_W, L1_gnn_W, L1_gnn_b, L1_gnn_C, L2_gnn_weight, L2_gnn_w_ih, L2_gnn_w_hh, L2_gnn_b_ih, L2_gnn_b_hh, L3_gnn_weight, L3_gnn_bias):
    import jax
    import jax.numpy as jnp

    def _L0_gnn_ref(matrix, mask, adj, W):
        import jax, jax.numpy as jnp
        import numpy as np
        HIDDEN = 128
        NEG_INF = -1e+30
        intermediate = jnp.einsum('bsh,hd->bsd', matrix, W)
        similarities = jnp.einsum('bsd,btd->bst', intermediate, matrix)
        similarities = similarities * adj
        key_mask = mask[:, None, :].astype(bool)
        masked = jnp.where(key_mask, similarities, NEG_INF)
        attn = jax.nn.softmax(masked, axis=-1)
        output = jnp.einsum('bst,bth->bsh', attn, matrix)
        return output

    def _L1_gnn_ref(x, adj, W, b, C):
        import jax, jax.numpy as jnp
        import numpy as np
        B, N, IN_DIM, OUT_DIM, H = (4, 1024, 128, 128, 8)
        ATN = OUT_DIM // H
        xt = jnp.einsum('bni,hio->bhno', x, W) + b[None, :, None, :]
        xC = jnp.einsum('bhno,hpo->bhnp', xt, C)
        scores = jnp.einsum('bhnp,bhmp->bhnm', xC, xt)
        alpha = jnp.tanh(scores * adj[:, None, :, :])
        heads = jnp.einsum('bhnm,bhmo->bhno', alpha, xt)
        out = jnp.transpose(heads, (0, 2, 1, 3)).reshape(x.shape[0], x.shape[1], -1)
        return out

    def _L2_gnn_ref(x, adj, mask, weight, w_ih, w_hh, b_ih, b_hh):
        import jax, jax.numpy as jnp
        import numpy as np
        B, N, D, C, L = (64, 256, 128, 128, 5)
        EDGE_P = 0.02

        def _gru_cell(m, h, w_ih, w_hh, b_ih, b_hh):
            gi = m @ w_ih.T + b_ih
            gh = h @ w_hh.T + b_hh
            i_r, i_z, i_n = jnp.split(gi, 3, axis=-1)
            h_r, h_z, h_n = jnp.split(gh, 3, axis=-1)
            r = jax.nn.sigmoid(i_r + h_r)
            z = jax.nn.sigmoid(i_z + h_z)
            n = jnp.tanh(i_n + r * h_n)
            return (1.0 - z) * n + z * h
        A = (adj != 0).astype(x.dtype)
        h = x
        for l in range(weight.shape[0]):
            m = jnp.einsum('bnd,de->bne', h, weight[l])
            agg = jnp.einsum('bij,bid->bjd', A, m)
            h = _gru_cell(agg, h, w_ih, w_hh, b_ih, b_hh)
        return h * mask[..., None]

    def _L3_gnn_ref(x, adj, weight, bias):
        import jax, jax.numpy as jnp
        import numpy as np
        support = jnp.einsum('bni,io->bno', x, weight)
        out = jnp.einsum('bnm,bmo->bno', adj, support)
        return out + bias
    h = jnp.maximum(_layernorm(x, axis=-1), 0.0)
    x = x + _L0_gnn_ref(h, nodemask, adj, L0_gnn_W)
    h = jnp.maximum(_layernorm(x, axis=-1), 0.0)
    x = x + _L1_gnn_ref(h, adj, L1_gnn_W, L1_gnn_b, L1_gnn_C)
    h = jnp.maximum(_layernorm(x, axis=-1), 0.0)
    x = x + _L2_gnn_ref(h, adj, nodemask, L2_gnn_weight, L2_gnn_w_ih, L2_gnn_w_hh, L2_gnn_b_ih, L2_gnn_b_hh)
    h = jnp.maximum(_layernorm(x, axis=-1), 0.0)
    x = x + _L3_gnn_ref(h, adj, L3_gnn_weight, L3_gnn_bias)
    return x

_drawn_inputs = setup_inputs


def setup_inputs(seed=0):
    import zlib

    import numpy as np

    out = dict(_drawn_inputs(seed))
    spreads = {}
    factors = {'L3_gnn_bias': 4.715}
    for name, (base, spread) in spreads.items():
        noise = np.random.default_rng([zlib.crc32(name.encode()), seed]).standard_normal(out[name].shape)
        drawn = base * np.exp(spread * noise) if base else spread * noise
        out[name] = jnp.asarray(drawn.astype(out[name].dtype))
    for name, factor in factors.items():
        out[name] = (out[name] * factor).astype(out[name].dtype)
    return out
```

```python
from contextlib import ExitStack

import concourse.bass as bass
from concourse import mybir

F32 = mybir.dt.float32
F32R = mybir.dt.float32r
I32 = mybir.dt.int32
ALU = mybir.AluOpType
ACT = mybir.ActivationFunctionType
X_AXIS = mybir.AxisListType.X

GRAPHS, NODES, FEAT = 128, 128, 128
GROUP = 4
SLOTS = 2
ROUNDS = GRAPHS // (GROUP * SLOTS)
WIDE = GROUP * NODES
HALF = GROUP // 2
HEADS, HEAD = 8, 16
PAD = 32
QUADS = 4
TILES = HEADS // QUADS
LAYERS = 5
NORMS = 4
NEG = -1e30
TOP = 3e38
EPS = 1e-5


class Slot:

    def __init__(self, n, sb, psum, sem):
        self.n = n

        def tile(name, dt=F32):
            return sb(f"{name}{n}", [128, GROUP, 128], dt)

        def done(name):
            return sem(f"s_{name}{n}")

        self.XIN = tile("XIN")
        self.ADJ = tile("ADJ")
        self.CAP = tile("CAP")
        self.X1 = tile("X1")
        self.X2 = tile("X2")
        self.X3 = tile("X3")
        self.X3B = tile("X3B")
        self.OUT = tile("OUT")
        self.HA = tile("HA")
        self.HAT = tile("HAT")
        self.IT = tile("IT")
        self.ZRAW = tile("ZRAW")
        self.Z = tile("Z")
        self.E = tile("E")
        self.ET = tile("ET")
        self.A01 = tile("A01")
        self.ADJT = tile("ADJT")
        self.XT = sb(f"XT{n}", [128, TILES, GROUP, 128])
        self.YT = sb(f"YT{n}", [128, TILES, GROUP, 128])
        self.XN = sb(f"XN{n}", [128, TILES, GROUP, 128])
        self.OT = sb(f"OT{n}", [128, TILES, GROUP, 128])
        self.SC = sb(f"SC{n}", [128, QUADS, HALF, TILES, 128])
        self.H = tile("H")
        self.HT = tile("HT")
        self.HTH = tile("HTH", F32R)
        self.HTL = tile("HTL", F32R)
        self.AGH = tile("AGH", F32R)
        self.AGL = tile("AGL", F32R)
        self.R = tile("R")
        self.ZG = tile("ZG")
        self.OMZ = tile("OMZ")
        self.ZH = tile("ZH")
        self.NG = tile("NG")
        self.T = tile("T")
        self.U = tile("U")
        self.Q = tile("Q")
        self.CV = tile("CV")
        self.STAT = sb(f"STAT{n}", [128, NORMS, GROUP, 6])
        self.COUNT = sb(f"COUNT{n}", [128, NORMS, GROUP])
        self.MV = sb(f"MV{n}", [128, NORMS, GROUP, 2])
        self.NMEAN = sb(f"NMEAN{n}", [128, NORMS, GROUP])
        self.VE = sb(f"VE{n}", [128, NORMS, GROUP])
        self.RSTD = sb(f"RSTD{n}", [128, NORMS, GROUP])
        self.SHIFT = sb(f"SHIFT{n}", [128, NORMS, GROUP])
        self.NMAX = sb(f"NMAX{n}", [128, GROUP])
        self.SUM = sb(f"SUM{n}", [128, GROUP])
        self.RSUM = sb(f"RSUM{n}", [128, GROUP])
        self.P = [psum(f"P{n}_{b}", [128, GROUP, 128], F32) for b in range(4)]

        self.s_x_in = done("x_in")
        self.s_adj_in = done("adj_in")
        self.s_cap_in = done("cap_in")
        self.s_out_done = done("out_done")
        self.s_stat = done("stat")
        self.s_mv = done("mv")
        self.s_ve = done("ve")
        self.s_rstd = done("rstd")
        self.s_shift = done("shift")
        self.s_ha = done("ha")
        self.s_h = done("h")
        self.s_adjt_ps = done("adjt_ps")
        self.s_adjt = done("adjt")
        self.s_a01 = done("a01")
        self.s_hat_ps = done("hat_ps")
        self.s_hat = done("hat")
        self.s_it_ps = done("it_ps")
        self.s_it = done("it")
        self.s_sim_ps = done("sim_ps")
        self.s_z_raw = done("z_raw")
        self.s_z = done("z")
        self.s_nmax = done("nmax")
        self.s_e = done("e")
        self.s_rsum = done("rsum")
        self.s_et_ps = done("et_ps")
        self.s_et = done("et")
        self.s_att_ps = done("att_ps")
        self.s_x1 = done("x1")
        self.s_xt_ps = done("xt_ps")
        self.s_xt = done("xt")
        self.s_xn_ps = done("xn_ps")
        self.s_xn = done("xn")
        self.s_yt_ps = done("yt_ps")
        self.s_yt = done("yt")
        self.s_sc_ps = done("sc_ps")
        self.s_sc = done("sc")
        self.s_alpha = done("alpha")
        self.s_heads_ps = done("heads_ps")
        self.s_ot = done("ot")
        self.s_ott_ps = done("ott_ps")
        self.s_x2 = done("x2")
        self.s_h2t_ps = done("h2t_ps")
        self.s_ht = done("ht")
        self.s_hth = done("hth")
        self.s_htl = done("htl")
        self.s_agg_ps = done("agg_ps")
        self.s_agh = done("agh")
        self.s_agl = done("agl")
        self.s_n_ps = done("n_ps")
        self.s_r_ps = done("r_ps")
        self.s_z_ps = done("z_ps")
        self.s_in_ps = done("in_ps")
        self.s_r = done("r")
        self.s_zg = done("zg")
        self.s_omz = done("omz")
        self.s_zh = done("zh")
        self.s_t = done("t")
        self.s_u = done("u")
        self.s_ng = done("ng")
        self.s_q = done("q")
        self.s_hn_ps = done("hn_ps")
        self.s_hn = done("hn")
        self.s_x3 = done("x3")
        self.s_x3b = done("x3b")
        self.s_cv_ps = done("cv_ps")
        self.s_cv = done("cv")
        self.s_out_ps = done("out_ps")
        self.s_out = done("out")


def build(nc, x, adj, mask, mask_t, w0, w1, b1, c1, w2t, wiht, whht, bih, bhh, w3, b3, cap_dram, out):
    ctx = ExitStack()
    with ctx:
        def sb(name, shape, dt=F32):
            return ctx.enter_context(nc.sbuf_tensor(name, shape, dt))

        def psum(name, shape, dt):
            return ctx.enter_context(nc.psum_tensor(name, shape, dt))

        def sem(name):
            return ctx.enter_context(nc.semaphore(name))

        W0 = sb("W0", [128, FEAT])
        W1 = sb("W1", [128, TILES, 128])
        B1 = sb("B1", [128, TILES])
        C1 = sb("C1", [128, TILES, 128])
        BIH = sb("BIH", [128, 3])
        BHH = sb("BHH", [128, 3])
        BRZ = sb("BRZ", [128, 3])
        NBZ = sb("NBZ", [128, 3])
        VH = sb("VH", [128, LAYERS, 3, FEAT], F32R)
        VL = sb("VL", [128, LAYERS, 3, FEAT], F32R)
        WHHH = sb("WHHH", [128, 3, FEAT], F32R)
        WHHL = sb("WHHL", [128, 3, FEAT], F32R)
        W3 = sb("W3", [128, FEAT])
        B3 = sb("B3", [128, FEAT])
        MASKT = sb("MASKT", [128, GRAPHS])
        IDENT = sb("IDENT", [128, 128])
        MINUS_HALF = sb("MINUS_HALF", [128, GROUP])
        EPSILON = sb("EPSILON", [128, GROUP])
        ZEROS = sb("ZEROS", [128, GROUP])

        s_weights = sem("s_weights")
        s_masks = sem("s_masks")
        s_zero = sem("s_zero")
        s_ident = sem("s_ident")
        s_half = sem("s_half")
        s_mask01 = sem("s_mask01")
        s_caps = sem("s_caps")
        s_caps_out = sem("s_caps_out")
        s_maskt = sem("s_maskt")
        s_brz = sem("s_brz")
        s_nbz = sem("s_nbz")
        s_v_ps = sem("s_v_ps")
        s_vh = sem("s_vh")
        s_vl = sem("s_vl")
        s_whhh = sem("s_whhh")
        s_whhl = sem("s_whhl")

        slots = [Slot(n, sb, psum, sem) for n in range(SLOTS)]
        first, second = slots

        ZERO = first.Q[:, 0, :]
        MASK = first.U[:, 0, :].bitcast(I32)
        MASK01 = first.U[:, 1, :]
        CAPS = first.U[:, 2, :]
        MASKT_I = first.U[:, 3, :].bitcast(I32)
        WIHT = first.SC[:, 0, :, :, :].rearrange("p a b n -> p (a b n)")[:, 0:3 * FEAT]
        WHHT = first.SC[:, 1, :, :, :].rearrange("p a b n -> p (a b) n")[:, 0:3, :]
        W2T = second.SC[:, 0:2, :, :, :].rearrange("p q a b n -> p (q a b) n")[:, 0:LAYERS, :]

        def after(eng, semaphore, n):
            if not isinstance(n, int) or n > 0:
                eng.wait_ge(semaphore, n)

        def pipeline(eng, phase):
            phase(first, 0, None, 0)
            phase(second, 0, first, 0)
            phase(first, 1, second, 0)
            with eng.Fori(1, ROUNDS - 1) as i:
                phase(second, i, first, i)
                phase(first, i + 1, second, i)
            phase(second, ROUNDS - 1, first, ROUNDS - 1)
            phase(first, ROUNDS, second, ROUNDS - 1)
            phase(second, ROUNDS, None, 0)

        N_WEIGHTS = 16 * 11

        def norm_index(norm, i):
            if norm == 0:
                return 0 if isinstance(i, int) and i == 0 else 4 * i - 1
            if norm == 3:
                return 4 * i + (3 if isinstance(i, int) and i == ROUNDS - 1 else 4)
            return 4 * i + norm

        block = ctx.enter_context(nc.Block())

        @block.sync
        def _(sp):
            def load(S, i):
                g = i * (SLOTS * GROUP) + S.n * GROUP
                after(sp, S.s_x1, i * GROUP)
                sp.dma_start(S.XIN[:, :, :],
                             x[bass.ds(g, GROUP), :, :].rearrange("b n d -> n b d"))\
                    .then_inc(S.s_x_in, 16)
                after(sp, S.s_z, i)
                after(sp, S.s_a01, i)
                after(sp, S.s_adjt_ps, i)
                sp.dma_start(S.ADJ[:, :, :],
                             adj[bass.ds(g, GROUP), :, :].rearrange("b n d -> n b d"))\
                    .then_inc(S.s_adj_in, 16)

            def load_cap(S, i):
                g = i * (SLOTS * GROUP) + S.n * GROUP
                sp.dma_start(S.CAP[:, :, :],
                             cap_dram[bass.ds(g, GROUP), :].partition_broadcast(128))\
                    .then_inc(S.s_cap_in, 16)

            def store(S, i):
                g = i * (SLOTS * GROUP) + S.n * GROUP
                sp.wait_ge(S.s_out, i + 1)
                sp.dma_start(out[bass.ds(g, GROUP), :, :].rearrange("b n d -> n b d"),
                             S.OUT[:, :, :]).then_inc(S.s_out_done, 16)

            load(first, 0)
            sp.dma_start(MASK, mask).then_inc(s_masks, 16)
            sp.dma_start(MASKT_I, mask_t).then_inc(s_masks, 16)
            for dst, src in [(W0[:, :], w0), (W1[:, :, :], w1), (B1[:, :], b1), (C1[:, :, :], c1),
                             (WHHT, whht), (WIHT, wiht), (W2T, w2t), (BIH[:, :], bih),
                             (BHH[:, :], bhh), (W3[:, :], w3), (B3[:, :], b3.partition_broadcast(128))]:
                sp.dma_start(dst, src).then_inc(s_weights, 16)
            load(second, 0)
            sp.wait_ge(s_caps, 1)
            sp.dma_start(cap_dram[:, :], CAPS).then_inc(s_caps_out, 16)
            sp.wait_ge(s_caps_out, 16)
            for S in slots:
                load_cap(S, 0)
            for S in slots:
                load(S, 1)
                load_cap(S, 1)
            with sp.Fori(2, ROUNDS) as i:
                for S in slots:
                    load(S, i)
                    load_cap(S, i)
                    store(S, i - 2)
            for i in (ROUNDS - 2, ROUNDS - 1):
                for S in slots:
                    store(S, i)
            for S in slots:
                sp.wait_ge(S.s_out_done, 16 * ROUNDS)

        @block.tensor
        def _(pe):
            pe.wait_ge(s_weights, N_WEIGHTS)
            for l in range(LAYERS):
                bank = (second.P + first.P[3:])[l].rearrange("p b n -> p (b n)")
                pe.matmul(bank[:, 0:3 * FEAT], W2T[:, l, :], WIHT, start=True, stop=True)\
                    .then_inc(s_v_ps, 1)
            pe.wait_ge(s_ident, 1)
            pe.wait_ge(s_vl, LAYERS)
            pe.wait_ge(s_whhl, 1)

            def turn(bank, src):
                for b in range(GROUP):
                    last = pe.transpose(bank[:, b, :], src[:, b, :], IDENT[:, :])
                return last


            def turn_ha(S, i, norm):
                pe.wait_ge(S.s_ha, GROUP * (2 * i + norm + 1))
                if norm == 0:
                    after(pe, S.s_x3, GROUP * i)
                turn(S.P[0 if norm == 0 else 3], S.HA).then_inc(S.s_hat_ps, 1)

            def inter(S, i):
                pe.wait_ge(S.s_hat, 2 * i + 1)
                pe.matmul(S.P[3][:, :, :], W0[:, :], S.HAT[:, :, :], start=True, stop=True)\
                    .then_inc(S.s_it_ps, 1)

            def similarities(S, i):
                pe.wait_ge(S.s_it, i + 1)
                for b in range(GROUP):
                    last = pe.matmul(S.P[0][:, b, :], S.IT[:, b, :], S.HAT[:, b, :],
                                     start=True, stop=True)
                last.then_inc(S.s_sim_ps, 1)

            def turn_e(S, i):
                pe.wait_ge(S.s_e, GROUP * (i + 1))
                turn(S.P[3], S.E).then_inc(S.s_et_ps, 1)

            def attend(S, i):
                pe.wait_ge(S.s_et, i + 1)
                for b in range(GROUP):
                    last = pe.matmul(S.P[0][:, b, :], S.ET[:, b, :], S.HA[:, b, :],
                                     start=True, stop=True)
                last.then_inc(S.s_att_ps, 1)

            def turn_adj(S, i):
                pe.wait_ge(S.s_adj_in, 16 * (i + 1))
                after(pe, S.s_cv, i)
                turn(S.P[1], S.ADJ).then_inc(S.s_adjt_ps, 1)

            def head_features(S, i):
                pe.wait_ge(S.s_hat, 2 * i + 2)
                pe.wait_ge(S.s_adjt, i + 1)
                after(pe, S.s_out, i)
                for t in range(TILES):
                    pe.matmul(S.P[1 + t][:, :, :], W1[:, t, :], S.HAT[:, :, :],
                              start=True, stop=True).then_inc(S.s_xt_ps, 1)

            def head_features_c(S, i):
                pe.wait_ge(S.s_xt, TILES * (i + 1))
                for t in range(TILES):
                    pe.matmul(S.P[1 + t][:, :, :], C1[:, t, :], S.XT[:, t, :, :],
                              start=True, stop=True).then_inc(S.s_yt_ps, 1)

            def turn_head_features(S, i):
                for t, bank in ((0, S.P[0]), (1, S.P[3])):
                    for b in range(GROUP):
                        last = pe.transpose(bank[:, b, :], S.XT[:, t, b, :], IDENT[:, :])
                    last.then_inc(S.s_xn_ps, 1)

            def scores(S, i, k):
                pe.wait_ge(S.s_yt, TILES * (i + 1))
                pe.wait_ge(S.s_xn, TILES * (i + 1))
                if k:
                    pe.wait_ge(S.s_ot, 2 * i + 1)
                for b in range(HALF):
                    for t in range(TILES):
                        for q in range(QUADS):
                            rows = slice(PAD * q, PAD * q + HEAD)
                            last = pe.matmul(S.P[q][:, TILES * b + t, :],
                                             S.XT[rows, t, HALF * k + b, :],
                                             S.YT[rows, t, HALF * k + b, :], start=True, stop=True)
                last.then_inc(S.s_sc_ps, 1)

            def heads(S, i, k):
                pe.wait_ge(S.s_alpha, QUADS * (2 * i + k + 1))
                for b in range(HALF):
                    for t in range(TILES):
                        for q in range(QUADS):
                            rows = slice(PAD * q, PAD * q + PAD)
                            last = pe.matmul(S.P[0][rows, HALF * t + b, :],
                                             S.XN[:, t, HALF * k + b, rows],
                                             S.SC[:, q, b, t, :], start=True, stop=True)
                last.then_inc(S.s_heads_ps, 1)

            def turn_heads(S, i, k):
                pe.wait_ge(S.s_ot, 2 * i + k + 1)
                if k == 0:
                    pe.wait_ge(S.s_sc, QUADS * (2 * i + 2))
                for b in range(HALF):
                    for t in range(TILES):
                        last = pe.transpose(S.P[1 + k][:, TILES * b + t, :],
                                            S.OT[:, t, HALF * k + b, :], IDENT[:, :])
                last.then_inc(S.s_ott_ps, 1)


            def turn_h2(S, i):
                pe.wait_ge(S.s_h, GROUP * (2 * i + 1))
                turn(S.P[0], S.H).then_inc(S.s_h2t_ps, 1)

            def hidden(bank, c, S):
                pe.matmul(bank[:, :, :], WHHH[:, c, :], S.HTH[:, :, :], start=True, stop=False)
                pe.matmul(bank[:, :, :], WHHL[:, c, :], S.HTH[:, :, :], start=False, stop=False)

            def gates_hidden(S, i, l):
                pe.wait_ge(S.s_hth, LAYERS * i + l + 1)
                hidden(S.P[2], 0, S)
                hidden(S.P[3], 1, S)
                if l == 0:
                    pe.wait_ge(S.s_a01, i + 1)
                    pe.wait_ge(S.s_ht, (LAYERS + 1) * i + 1)
                else:
                    pe.wait_ge(S.s_hn, (LAYERS - 1) * i + l)
                for b in range(GROUP):
                    last = pe.matmul(S.P[0][:, b, :], S.H[:, b, :], S.A01[:, b, :],
                                     start=True, stop=True)
                last.then_inc(S.s_agg_ps, 1)
                hidden(S.P[1], 2, S)
                pe.wait_ge(S.s_htl, LAYERS * i + l + 1)
                pe.matmul(S.P[1][:, :, :], WHHH[:, 2, :], S.HTL[:, :, :], start=False, stop=True)\
                    .then_inc(S.s_n_ps, 1)
                pe.matmul(S.P[2][:, :, :], WHHH[:, 0, :], S.HTL[:, :, :], start=False, stop=False)
                pe.matmul(S.P[3][:, :, :], WHHH[:, 1, :], S.HTL[:, :, :], start=False, stop=False)

            def gates_input(S, i, l):
                pe.wait_ge(S.s_agh, LAYERS * i + l + 1)
                for c in (0, 1):
                    bank = S.P[2 + c]
                    pe.matmul(bank[:, :, :], VH[:, l, c, :], S.AGH[:, :, :], start=False, stop=False)
                    pe.matmul(bank[:, :, :], VL[:, l, c, :], S.AGH[:, :, :], start=False, stop=False)
                pe.wait_ge(S.s_agl, LAYERS * i + l + 1)
                pe.matmul(S.P[2][:, :, :], VH[:, l, 0, :], S.AGL[:, :, :], start=False, stop=True)\
                    .then_inc(S.s_r_ps, 1)
                pe.matmul(S.P[3][:, :, :], VH[:, l, 1, :], S.AGL[:, :, :], start=False, stop=True)\
                    .then_inc(S.s_z_ps, 1)
                pe.matmul(S.P[0][:, :, :], VH[:, l, 2, :], S.AGH[:, :, :], start=True, stop=False)
                pe.matmul(S.P[0][:, :, :], VL[:, l, 2, :], S.AGH[:, :, :], start=False, stop=False)
                pe.matmul(S.P[0][:, :, :], VH[:, l, 2, :], S.AGL[:, :, :], start=False, stop=True)\
                    .then_inc(S.s_in_ps, 1)

            def turn_new(S, i, l):
                pe.wait_ge(S.s_ht, (LAYERS + 1) * i + l + 2)
                turn(S.P[0], S.HT).then_inc(S.s_hn_ps, 1)


            def conv(S, i):
                pe.wait_ge(S.s_h, GROUP * (2 * i + 2))
                for b in range(GROUP):
                    last = pe.matmul(S.P[1][:, b, :], S.H[:, b, :], S.ADJT[:, b, :],
                                     start=True, stop=True)
                last.then_inc(S.s_cv_ps, 1)

            def conv_out(S, i):
                pe.wait_ge(S.s_cv, i + 1)
                for b in range(GROUP):
                    last = pe.matmul(S.P[2][:, b, :], S.CV[:, b, :], W3[:, :],
                                     start=True, stop=True)
                last.then_inc(S.s_out_ps, 1)

            def phase(F, f, B, b):
                old = not isinstance(f, int) or f > 0
                new = not isinstance(f, int) or f < ROUNDS
                if new:
                    turn_ha(F, f, 0)
                if B:
                    turn_h2(B, b)
                if new:
                    inter(F, f)
                if B:
                    gates_hidden(B, b, 0)
                if new:
                    similarities(F, f)
                if B:
                    gates_input(B, b, 0)
                if old:
                    conv(F, f - 1)
                if new:
                    turn_e(F, f)
                if old:
                    conv_out(F, f - 1)
                if B:
                    turn_new(B, b, 0)
                    gates_hidden(B, b, 1)
                if new:
                    attend(F, f)
                if B:
                    gates_input(B, b, 1)
                if new:
                    turn_adj(F, f)
                if B:
                    turn_new(B, b, 1)
                    gates_hidden(B, b, 2)
                if new:
                    turn_ha(F, f, 1)
                if B:
                    gates_input(B, b, 2)
                if new:
                    head_features(F, f)
                    head_features_c(F, f)
                if B:
                    turn_new(B, b, 2)
                    gates_hidden(B, b, 3)
                if new:
                    turn_head_features(F, f)
                    scores(F, f, 0)
                if B:
                    gates_input(B, b, 3)
                if new:
                    heads(F, f, 0)
                if B:
                    turn_new(B, b, 3)
                    gates_hidden(B, b, 4)
                if new:
                    scores(F, f, 1)
                if B:
                    gates_input(B, b, 4)
                if new:
                    heads(F, f, 1)
                    turn_heads(F, f, 0)
                    turn_heads(F, f, 1)
                if B:
                    turn_new(B, b, 4)

            pipeline(pe, phase)

        @block.scalar
        def _(act):
            act.wait_ge(s_weights, N_WEIGHTS)
            act.wait_ge(s_brz, 1)
            act.wait_ge(s_nbz, 1)

            def normed(S, i, norm):
                src = (S.XIN, S.X1, S.X2, S.X3)[norm]
                dst, done = ((S.HA, S.s_ha), (S.HA, S.s_ha), (S.H, S.s_h), (S.H, S.s_h))[norm]
                act.wait_ge(S.s_shift, norm_index(norm, i) + 1)
                for b in range(GROUP):
                    act.activation(dst[:, b, :], src[:, b, :], ACT.Relu,
                                   bias=S.SHIFT[:, norm, b:b + 1], scale=S.RSTD[:, norm, b:b + 1])\
                        .then_inc(done, 1)

            def adj_t(S, i):
                act.wait_ge(S.s_adjt_ps, i + 1)
                act.copy(S.ADJT[:, :, :], S.P[1][:, :, :]).then_inc(S.s_adjt, 1)

            def ha_t(S, i, norm):
                act.wait_ge(S.s_hat_ps, 2 * i + norm + 1)
                act.copy(S.HAT[:, :, :], S.P[0 if norm == 0 else 3][:, :, :]).then_inc(S.s_hat, 1)

            def exps(S, i):
                act.wait_ge(S.s_nmax, i + 1)
                for b in range(GROUP):
                    act.activation(S.E[:, b, :], S.Z[:, b, :], ACT.Exp,
                                   bias=S.NMAX[:, b:b + 1], accum_out=S.SUM[:, b:b + 1])\
                        .then_inc(S.s_e, 1)

            def e_t(S, i):
                act.wait_ge(S.s_et_ps, i + 1)
                act.copy(S.ET[:, :, :], S.P[3][:, :, :]).then_inc(S.s_et, 1)

            def features(S, i):
                for t in range(TILES):
                    act.wait_ge(S.s_xt_ps, TILES * i + t + 1)
                    act.activation(S.XT[:, t, :, :], S.P[1 + t][:, :, :], ACT.Identity,
                                   bias=B1[:, t:t + 1]).then_inc(S.s_xt, 1)

            def features_c(S, i):
                for t in range(TILES):
                    act.wait_ge(S.s_yt_ps, TILES * i + t + 1)
                    act.copy(S.YT[:, t, :, :], S.P[1 + t][:, :, :]).then_inc(S.s_yt, 1)

            def features_natural(S, i):
                for t, bank in ((0, S.P[0]), (1, S.P[3])):
                    act.wait_ge(S.s_xn_ps, TILES * i + t + 1)
                    act.copy(S.XN[:, t, :, :], bank[:, :, :]).then_inc(S.s_xn, 1)

            def tanhs(S, i, k):
                for q in range(QUADS):
                    act.wait_ge(S.s_sc, QUADS * (2 * i + k) + q + 1)
                    act.activation(S.SC[:, q, :, :, :], S.SC[:, q, :, :, :], ACT.Tanh)\
                        .then_inc(S.s_alpha, 1)

            def h_t(S, i):
                act.wait_ge(S.s_h2t_ps, i + 1)
                act.copy(S.HTH[:, :, :], S.P[0][:, :, :]).then_inc(S.s_hth, 1)
                act.copy(S.HT[:, :, :], S.P[0][:, :, :]).then_inc(S.s_ht, 1)

            def h_high(S, i, l):
                act.wait_ge(S.s_ht, (LAYERS + 1) * i + l + 1)
                act.copy(S.HTH[:, :, :], S.HT[:, :, :]).then_inc(S.s_hth, 1)

            def aggregated(S, i, l):
                act.wait_ge(S.s_agg_ps, LAYERS * i + l + 1)
                act.copy(S.AGH[:, :, :], S.P[0][:, :, :]).then_inc(S.s_agh, 1)

            def gates(S, i, l):
                act.wait_ge(S.s_r_ps, LAYERS * i + l + 1)
                act.activation(S.R[:, :, :], S.P[2][:, :, :], ACT.Sigmoid, bias=BRZ[:, 0:1])\
                    .then_inc(S.s_r, 1)
                act.wait_ge(S.s_z_ps, LAYERS * i + l + 1)
                act.activation(S.ZG[:, :, :], S.P[3][:, :, :], ACT.Sigmoid, bias=BRZ[:, 1:2])\
                    .then_inc(S.s_zg, 1)

            def gate_n(S, i, l):
                act.wait_ge(S.s_u, LAYERS * i + l + 1)
                act.activation(S.NG[:, :, :], S.U[:, :, :], ACT.Tanh, bias=BIH[:, 2:3])\
                    .then_inc(S.s_ng, 1)

            def h_natural(S, i, l):
                act.wait_ge(S.s_hn_ps, LAYERS * i + l + 1)
                act.copy(S.H[:, :, :], S.P[0][:, :, :]).then_inc(S.s_hn, 1)

            def conved(S, i):
                act.wait_ge(S.s_cv_ps, i + 1)
                act.copy(S.CV[:, :, :], S.P[1][:, :, :]).then_inc(S.s_cv, 1)

            for S in slots:
                normed(S, 0, 0)

            def phase(F, f, B, b):
                old = not isinstance(f, int) or f > 0
                new = not isinstance(f, int) or f < ROUNDS
                ahead = B and (not isinstance(b, int) or b + 1 < ROUNDS)
                if new:
                    ha_t(F, f, 0)
                if B:
                    h_t(B, b)
                if old:
                    normed(F, f - 1, 3)
                if B:
                    aggregated(B, b, 0)
                    gates(B, b, 0)
                if new:
                    exps(F, f)
                if old:
                    conved(F, f - 1)
                if B:
                    gate_n(B, b, 0)
                if new:
                    e_t(F, f)
                if B:
                    h_high(B, b, 1)
                    h_natural(B, b, 0)
                    aggregated(B, b, 1)
                    gates(B, b, 1)
                if new:
                    adj_t(F, f)
                if B:
                    gate_n(B, b, 1)
                if new:
                    normed(F, f, 1)
                if B:
                    h_high(B, b, 2)
                    h_natural(B, b, 1)
                if new:
                    ha_t(F, f, 1)
                if B:
                    aggregated(B, b, 2)
                    gates(B, b, 2)
                if new:
                    features(F, f)
                if B:
                    gate_n(B, b, 2)
                if new:
                    features_c(F, f)
                if B:
                    h_high(B, b, 3)
                    h_natural(B, b, 2)
                if new:
                    features_natural(F, f)
                if B:
                    aggregated(B, b, 3)
                    gates(B, b, 3)
                if new:
                    tanhs(F, f, 0)
                if B:
                    gate_n(B, b, 3)
                    h_high(B, b, 4)
                    h_natural(B, b, 3)
                    aggregated(B, b, 4)
                    gates(B, b, 4)
                if new:
                    tanhs(F, f, 1)
                if B:
                    gate_n(B, b, 4)
                if ahead:
                    normed(B, b + 1, 0)
                if new:
                    normed(F, f, 2)

            pipeline(act, phase)

        @block.gpsimd
        def _(pool):
            pool.memset(ZERO, 0.0).then_inc(s_zero, 1)
            pool.memset(MINUS_HALF[:, :], -0.5).then_inc(s_half, 1)
            pool.memset(EPSILON[:, :], EPS).then_inc(s_half, 1)
            pool.memset(ZEROS[:, :], 0.0).then_inc(s_half, 1)
            pool.wait_ge(s_zero, 1)
            pool.affine_select(out=IDENT[:, :], in_=ZERO, compare_op=ALU.not_equal, fill=1.0,
                               base=0, pattern=[[-1, 128]], channel_multiplier=1)\
                .then_inc(s_ident, 1)
            pool.wait_ge(s_half, 3)
            pool.wait_ge(s_weights, N_WEIGHTS)
            pool.wait_ge(s_ident, 1)

            def scales(S, i, norm):
                n = norm_index(norm, i)
                pool.wait_ge(S.s_mv, GROUP * (n + 1))
                pool.tensor_tensor(S.VE[:, norm, :], S.MV[:, norm, :, 1], EPSILON[:, :], ALU.add)\
                    .then_inc(S.s_ve, 1)
                pool.tensor_tensor(S.NMEAN[:, norm, :], ZEROS[:, :], S.MV[:, norm, :, 0],
                                   ALU.subtract).then_inc(S.s_ve, 1)
                pool.wait_ge(S.s_ve, 2 * (n + 1))
                pool.tensor_tensor(S.RSTD[:, norm, :], S.VE[:, norm, :], MINUS_HALF[:, :], ALU.pow)\
                    .then_inc(S.s_rstd, 1)
                pool.wait_ge(S.s_rstd, n + 1)
                pool.tensor_tensor(S.SHIFT[:, norm, :], S.NMEAN[:, norm, :], S.RSTD[:, norm, :],
                                   ALU.mult).then_inc(S.s_shift, 1)

            def h_low(S, i, l):
                pool.wait_ge(S.s_ht, (LAYERS + 1) * i + l + 1)
                pool.wait_ge(S.s_hth, LAYERS * i + l + 1)
                pool.tensor_tensor(S.HTL[:, :, :], S.HT[:, :, :], S.HTH[:, :, :].bitcast(F32),
                                   ALU.subtract).then_inc(S.s_htl, 1)

            def mix(S, i, l):
                pool.wait_ge(S.s_zg, LAYERS * i + l + 1)
                pool.tensor_tensor(S.ZH[:, :, :], S.ZG[:, :, :], S.HT[:, :, :], ALU.mult)\
                    .then_inc(S.s_zh, 1)

            def bias_out(S, i):
                pool.wait_ge(S.s_x3, GROUP * (i + 1))
                pool.tensor_tensor(S.X3B[:, :, :], S.X3[:, :, :],
                                   B3[:, :].unsqueeze(1).to_broadcast([128, GROUP, FEAT]),
                                   ALU.add).then_inc(S.s_x3b, 1)

            for S in slots:
                scales(S, 0, 0)

            def phase(F, f, B, b):
                old = not isinstance(f, int) or f > 0
                new = not isinstance(f, int) or f < ROUNDS
                ahead = B and (not isinstance(b, int) or b + 1 < ROUNDS)
                if old:
                    scales(F, f - 1, 3)
                if B:
                    h_low(B, b, 0)
                if old:
                    bias_out(F, f - 1)
                if B:
                    mix(B, b, 0)
                    h_low(B, b, 1)
                    mix(B, b, 1)
                if new:
                    scales(F, f, 1)
                if B:
                    for l in range(2, LAYERS):
                        h_low(B, b, l)
                        mix(B, b, l)
                if ahead:
                    scales(B, b + 1, 0)
                if new:
                    scales(F, f, 2)

            pipeline(pool, phase)

        @block.vector
        def _(dve):
            dve.wait_ge(s_masks, 32)
            dve.tensor_scalar(MASK01, MASK, 0.0, None, ALU.not_equal).then_inc(s_mask01, 1)
            dve.tensor_copy(MASKT[:, :], MASKT_I).then_inc(s_maskt, 1)
            dve.wait_ge(s_mask01, 1)
            dve.tensor_scalar(CAPS, MASK01, TOP, NEG, ALU.mult, ALU.add).then_inc(s_caps, 1)
            dve.wait_ge(s_weights, N_WEIGHTS)
            dve.tensor_tensor(BRZ[:, :], BIH[:, :], BHH[:, :], ALU.add).then_inc(s_brz, 1)
            dve.wait_ge(s_brz, 1)
            dve.tensor_scalar(NBZ[:, :], BRZ[:, :], -1.0, None, ALU.mult).then_inc(s_nbz, 1)
            dve.tensor_copy(WHHH[:, :, :], WHHT).then_inc(s_whhh, 1)
            dve.wait_ge(s_whhh, 1)
            dve.tensor_tensor(WHHL[:, :, :], WHHT, WHHH[:, :, :].bitcast(F32), ALU.subtract)\
                .then_inc(s_whhl, 1)
            for l in range(LAYERS):
                dve.wait_ge(s_v_ps, l + 1)
                bank = (second.P + first.P[3:])[l]
                dve.tensor_copy(VH[:, l, :, :], bank[:, 0:3, :]).then_inc(s_vh, 1)
                dve.wait_ge(s_vh, l + 1)
                dve.tensor_tensor(VL[:, l, :, :], bank[:, 0:3, :], VH[:, l, :, :].bitcast(F32),
                                  ALU.subtract).then_inc(s_vl, 1)
            dve.wait_ge(s_maskt, 1)
            dve.wait_ge(s_whhl, 1)
            dve.wait_ge(s_caps_out, 16)

            def stats(S, i, norm):
                src = (S.XIN, S.X1, S.X2, S.X3)[norm]
                n = norm_index(norm, i)
                if norm == 0:
                    dve.wait_ge(S.s_x_in, 16 * (i + 1))
                elif norm == 1:
                    dve.wait_ge(S.s_x1, GROUP * (i + 1))
                elif norm == 2:
                    dve.wait_ge(S.s_x2, 2 * (i + 1))
                else:
                    dve.wait_ge(S.s_x3, GROUP * (i + 1))
                for b in range(GROUP):
                    dve.bn_stats(S.STAT[:, norm, b, :], src[:, b, :]).then_inc(S.s_stat, 1)
                dve.wait_ge(S.s_stat, (GROUP + 1) * n + GROUP)
                dve.tensor_copy(S.COUNT[:, norm, :], S.STAT[:, norm, :, 0]).then_inc(S.s_stat, 1)
                for b in range(GROUP):
                    dve.bn_aggr(S.MV[:, norm, b, :], S.STAT[:, norm, b, :]).then_inc(S.s_mv, 1)

            def adj_nonzero(S, i):
                dve.wait_ge(S.s_adj_in, 16 * (i + 1))
                dve.tensor_scalar(S.A01[:, :, :], S.ADJ[:, :, :], 0.0, None, ALU.not_equal)\
                    .then_inc(S.s_a01, 1)

            def inter(S, i):
                dve.wait_ge(S.s_it_ps, i + 1)
                dve.tensor_copy(S.IT[:, :, :], S.P[3][:, :, :]).then_inc(S.s_it, 1)

            def masked(S, i):
                dve.wait_ge(S.s_sim_ps, i + 1)
                dve.wait_ge(S.s_adj_in, 16 * (i + 1))
                dve.tensor_tensor(S.ZRAW[:, :, :], S.P[0][:, :, :], S.ADJ[:, :, :], ALU.mult)\
                    .then_inc(S.s_z_raw, 1)
                dve.wait_ge(S.s_z_raw, i + 1)
                dve.wait_ge(S.s_cap_in, 16 * (i + 1))
                dve.tensor_tensor(S.Z[:, :, :], S.ZRAW[:, :, :], S.CAP[:, :, :], ALU.min)\
                    .then_inc(S.s_z, 1)
                dve.wait_ge(S.s_z, i + 1)
                dve.tensor_reduce(S.NMAX[:, :], S.Z[:, :, :], X_AXIS, ALU.max, negate=True)\
                    .then_inc(S.s_nmax, 1)

            def add_attention(S, i):
                dve.wait_ge(S.s_e, GROUP * (i + 1))
                dve.reciprocal(S.RSUM[:, :], S.SUM[:, :]).then_inc(S.s_rsum, 1)
                dve.wait_ge(S.s_rsum, i + 1)
                dve.wait_ge(S.s_att_ps, i + 1)
                for b in range(GROUP):
                    dve.scalar_tensor_tensor(out=S.X1[:, b, :], in0=S.P[0][:, b, :],
                                             scalar=S.RSUM[:, b:b + 1], in1=S.XIN[:, b, :],
                                             op0=ALU.mult, op1=ALU.add).then_inc(S.s_x1, 1)

            def weigh_scores(S, i, k):
                dve.wait_ge(S.s_sc_ps, 2 * i + k + 1)
                both = S.ADJT[:, HALF * k:HALF * k + HALF, :].unsqueeze(2)\
                    .to_broadcast([128, HALF, TILES, 128])
                for q in range(QUADS):
                    bank = S.P[q][:, :, :].rearrange("p (b t) n -> p b t n", t=TILES)
                    dve.tensor_tensor(S.SC[:, q, :, :, :], bank, both, ALU.mult)\
                        .then_inc(S.s_sc, 1)

            def heads_out(S, i, k):
                dve.wait_ge(S.s_heads_ps, 2 * i + k + 1)
                bank = S.P[0][:, :, :].rearrange("p (t b) n -> p t b n", b=HALF)
                dve.tensor_copy(S.OT[:, :, HALF * k:HALF * k + HALF, :], bank)\
                    .then_inc(S.s_ot, 1)

            def add_heads(S, i, k):
                dve.wait_ge(S.s_ott_ps, 2 * i + k + 1)
                graphs = slice(HALF * k, HALF * k + HALF)
                real = S.P[1 + k][:, :, :].rearrange("p (b t) (q w) -> p b (t q) w",
                                                     t=TILES, w=PAD)[:, :, :, 0:HEAD]
                dve.tensor_tensor(
                    S.X2[:, graphs, :].rearrange("p b (h w) -> p b h w", w=HEAD), real,
                    S.X1[:, graphs, :].rearrange("p b (h w) -> p b h w", w=HEAD), ALU.add)\
                    .then_inc(S.s_x2, 1)

            def aggregate_low(S, i, l):
                dve.wait_ge(S.s_agh, LAYERS * i + l + 1)
                dve.tensor_tensor(S.AGL[:, :, :], S.P[0][:, :, :], S.AGH[:, :, :].bitcast(F32),
                                  ALU.subtract).then_inc(S.s_agl, 1)

            def reset(S, i, l):
                dve.wait_ge(S.s_n_ps, LAYERS * i + l + 1)
                dve.wait_ge(S.s_r, LAYERS * i + l + 1)
                dve.scalar_tensor_tensor(out=S.T[:, :, :], in0=S.P[1][:, :, :],
                                         scalar=BHH[:, 2:3], in1=S.R[:, :, :],
                                         op0=ALU.add, op1=ALU.mult).then_inc(S.s_t, 1)

            def step(S, i, l):
                dve.wait_ge(S.s_zg, LAYERS * i + l + 1)
                dve.tensor_scalar(S.OMZ[:, :, :], S.ZG[:, :, :], -1.0, 1.0, ALU.mult, ALU.add)\
                    .then_inc(S.s_omz, 1)
                dve.wait_ge(S.s_t, LAYERS * i + l + 1)
                dve.wait_ge(S.s_in_ps, LAYERS * i + l + 1)
                dve.tensor_tensor(S.U[:, :, :], S.P[0][:, :, :], S.T[:, :, :], ALU.add)\
                    .then_inc(S.s_u, 1)
                dve.wait_ge(S.s_omz, LAYERS * i + l + 1)
                dve.wait_ge(S.s_ng, LAYERS * i + l + 1)
                dve.tensor_tensor(S.Q[:, :, :], S.NG[:, :, :], S.OMZ[:, :, :], ALU.mult)\
                    .then_inc(S.s_q, 1)
                dve.wait_ge(S.s_zh, LAYERS * i + l + 1)
                dve.wait_ge(S.s_q, LAYERS * i + l + 1)
                dve.tensor_tensor(S.HT[:, :, :], S.Q[:, :, :], S.ZH[:, :, :], ALU.add)\
                    .then_inc(S.s_ht, 1)

            def add_hidden(S, i):
                dve.wait_ge(S.s_hn_ps, LAYERS * (i + 1))
                for b in range(GROUP):
                    graph = i * (SLOTS * GROUP) + S.n * GROUP + b
                    dve.scalar_tensor_tensor(out=S.X3[:, b, :], in0=S.P[0][:, b, :],
                                             scalar=MASKT[:, bass.ds(graph, 1)],
                                             in1=S.X2[:, b, :],
                                             op0=ALU.mult, op1=ALU.add).then_inc(S.s_x3, 1)

            def result(S, i):
                dve.wait_ge(S.s_out_ps, i + 1)
                dve.wait_ge(S.s_x3b, i + 1)
                after(dve, S.s_out_done, 16 * i)
                dve.tensor_tensor(S.OUT[:, :, :], S.P[2][:, :, :], S.X3B[:, :, :], ALU.add)\
                    .then_inc(S.s_out, 1)

            for S in slots:
                stats(S, 0, 0)

            def phase(F, f, B, b):
                old = not isinstance(f, int) or f > 0
                new = not isinstance(f, int) or f < ROUNDS
                ahead = B and (not isinstance(b, int) or b + 1 < ROUNDS)
                if old:
                    add_hidden(F, f - 1)
                    stats(F, f - 1, 3)
                if new:
                    inter(F, f)
                if B:
                    aggregate_low(B, b, 0)
                if new:
                    masked(F, f)
                if B:
                    reset(B, b, 0)
                    step(B, b, 0)
                if old:
                    result(F, f - 1)
                if B:
                    aggregate_low(B, b, 1)
                if new:
                    add_attention(F, f)
                    stats(F, f, 1)
                if B:
                    reset(B, b, 1)
                    step(B, b, 1)
                if new:
                    adj_nonzero(F, f)
                if B:
                    aggregate_low(B, b, 2)
                    reset(B, b, 2)
                    step(B, b, 2)
                    aggregate_low(B, b, 3)
                if ahead:
                    stats(B, b + 1, 0)
                if new:
                    weigh_scores(F, f, 0)
                if B:
                    reset(B, b, 3)
                    step(B, b, 3)
                if new:
                    heads_out(F, f, 0)
                if B:
                    aggregate_low(B, b, 4)
                if new:
                    weigh_scores(F, f, 1)
                if B:
                    reset(B, b, 4)
                    step(B, b, 4)
                if new:
                    heads_out(F, f, 1)
                    add_heads(F, f, 0)
                    add_heads(F, f, 1)
                    stats(F, f, 2)

            pipeline(dve, phase)


def kernel(x, adj, nodemask, L0_gnn_W, L1_gnn_W, L1_gnn_b, L1_gnn_C, L2_gnn_weight, L2_gnn_w_ih,
           L2_gnn_w_hh, L2_gnn_b_ih, L2_gnn_b_hh, L3_gnn_weight, L3_gnn_bias):
    import numpy as np
    import concourse.bacc as bacc
    from concourse.bass_utils import run_bass_kernel_spmd

    f = lambda a: np.ascontiguousarray(a)
    W, b, C = (np.asarray(a) for a in (L1_gnn_W, L1_gnn_b, L1_gnn_C))
    w1 = np.zeros((FEAT, TILES, QUADS, PAD), W.dtype)
    w1[:, :, :, :HEAD] = W.transpose(1, 0, 2).reshape(FEAT, TILES, QUADS, HEAD)
    b1 = np.zeros((QUADS, PAD, TILES), b.dtype)
    b1[:, :HEAD, :] = b.reshape(TILES, QUADS, HEAD).transpose(1, 2, 0)
    c1 = np.zeros((QUADS, PAD, TILES, QUADS, PAD), C.dtype)
    for h in range(HEADS):
        t, q = h // QUADS, h % QUADS
        c1[q, :HEAD, t, q, :HEAD] = C[h].T
    arrays = {
        "x": f(x), "adj": f(adj), "mask": f(nodemask), "mask_t": f(np.asarray(nodemask).T),
        "w0": f(L0_gnn_W), "w1": f(w1.reshape(FEAT, TILES, 128)), "b1": f(b1.reshape(128, TILES)),
        "c1": f(c1.reshape(128, TILES, 128)),
        "w2t": f(np.asarray(L2_gnn_weight).transpose(2, 0, 1)),
        "wiht": f(np.asarray(L2_gnn_w_ih).T),
        "whht": f(np.asarray(L2_gnn_w_hh).T.reshape(FEAT, 3, FEAT)),
        "bih": f(np.asarray(L2_gnn_b_ih).reshape(3, FEAT).T),
        "bhh": f(np.asarray(L2_gnn_b_hh).reshape(3, FEAT).T),
        "w3": f(L3_gnn_weight), "b3": f(L3_gnn_bias),
    }
    nc = bacc.Bacc("TRN2", target_bir_lowering=False, num_devices=1)
    args = {k: nc.dram_tensor(f"in_{k}", a.shape, mybir.dt.from_np(a.dtype), kind="ExternalInput").ap()
            for k, a in arrays.items()}
    cap_dram = nc.dram_tensor("cap_dram", (GRAPHS, NODES), F32, kind="Internal").ap()
    out = nc.dram_tensor("out_0", (GRAPHS, NODES, FEAT), F32, kind="ExternalOutput").ap()
    build(nc, cap_dram=cap_dram, out=out, **args)
    r = run_bass_kernel_spmd(nc, [{f"in_{k}": a for k, a in arrays.items()}], core_ids=[0])
    return r.results[0]["out_0"]
```

```python
from contextlib import ExitStack

import concourse.bass as bass
from concourse import mybir

F32 = mybir.dt.float32
F32R = mybir.dt.float32r
I32 = mybir.dt.int32
ALU = mybir.AluOpType
ACT = mybir.ActivationFunctionType
X_AXIS = mybir.AxisListType.X

GRAPHS, NODES, FEAT = 128, 128, 128
GROUP = 4
SLOTS = 2
ROUNDS = GRAPHS // (GROUP * SLOTS)
LAG = 2
WIDE = GROUP * NODES
HALF = GROUP // 2
HEADS, HEAD = 8, 16
PAD = 32
QUADS = 4
TILES = HEADS // QUADS
LAYERS = 5
NORMS = 4
NEG = -1e30
TOP = 3e38
EPS = 1e-5


class Slot:

    def __init__(self, n, sb, psum, sem):
        self.n = n

        def tile(name, dt=F32):
            return sb(f"{name}{n}", [128, GROUP, 128], dt)

        def done(name):
            return sem(f"s_{name}{n}")

        self.XIN = tile("XIN")
        self.ADJ = tile("ADJ")
        self.CAP = tile("CAP")
        self.X1 = tile("X1")
        self.X2 = tile("X2")
        self.X3 = tile("X3")
        self.X3B = tile("X3B")
        self.OUT = tile("OUT")
        self.HA = tile("HA")
        self.HAT = tile("HAT")
        self.IT = tile("IT")
        self.ZRAW = tile("ZRAW")
        self.Z = tile("Z")
        self.E = tile("E")
        self.ET = tile("ET")
        self.A01 = tile("A01")
        self.ADJT = tile("ADJT")
        self.XT = sb(f"XT{n}", [128, TILES, GROUP, 128])
        self.YT = sb(f"YT{n}", [128, TILES, GROUP, 128])
        self.XN = sb(f"XN{n}", [128, TILES, GROUP, 128])
        self.OT = sb(f"OT{n}", [128, TILES, GROUP, 128])
        self.SC = sb(f"SC{n}", [128, QUADS, HALF, TILES, 128])
        self.H = tile("H")
        self.HT = tile("HT")
        self.HTH = tile("HTH", F32R)
        self.HTL = tile("HTL", F32R)
        self.AGH = tile("AGH", F32R)
        self.AGL = tile("AGL", F32R)
        self.R = tile("R")
        self.ZG = tile("ZG")
        self.OMZ = tile("OMZ")
        self.ZH = tile("ZH")
        self.NG = tile("NG")
        self.T = tile("T")
        self.U = tile("U")
        self.Q = tile("Q")
        self.CV = tile("CV")
        self.STAT = sb(f"STAT{n}", [128, NORMS, GROUP, 6])
        self.COUNT = sb(f"COUNT{n}", [128, NORMS, GROUP])
        self.MV = sb(f"MV{n}", [128, NORMS, GROUP, 2])
        self.NMEAN = sb(f"NMEAN{n}", [128, NORMS, GROUP])
        self.VE = sb(f"VE{n}", [128, NORMS, GROUP])
        self.RSTD = sb(f"RSTD{n}", [128, NORMS, GROUP])
        self.SHIFT = sb(f"SHIFT{n}", [128, NORMS, GROUP])
        self.NMAX = sb(f"NMAX{n}", [128, GROUP])
        self.SUM = sb(f"SUM{n}", [128, GROUP])
        self.RSUM = sb(f"RSUM{n}", [128, GROUP])
        self.P = [psum(f"P{n}_{b}", [128, GROUP, 128], F32) for b in range(4)]

        self.s_x_in = done("x_in")
        self.s_adj_in = done("adj_in")
        self.s_cap_in = done("cap_in")
        self.s_out_done = done("out_done")
        self.s_rows_x = done("rows_x")
        self.s_rows = done("rows")
        self.s_scale_x = done("scale_x")
        self.s_scale = done("scale")
        self.s_ha = done("ha")
        self.s_h = done("h")
        self.s_adjt_ps = done("adjt_ps")
        self.s_adjt = done("adjt")
        self.s_a01 = done("a01")
        self.s_hat_ps = done("hat_ps")
        self.s_hat = done("hat")
        self.s_it_ps = done("it_ps")
        self.s_it = done("it")
        self.s_sim_ps = done("sim_ps")
        self.s_z_raw = done("z_raw")
        self.s_z = done("z")
        self.s_nmax = done("nmax")
        self.s_e = done("e")
        self.s_rsum = done("rsum")
        self.s_et_ps = done("et_ps")
        self.s_et = done("et")
        self.s_att_ps = done("att_ps")
        self.s_x1 = done("x1")
        self.s_xt_ps = done("xt_ps")
        self.s_xt = done("xt")
        self.s_xn_ps = done("xn_ps")
        self.s_xn = done("xn")
        self.s_yt_ps = done("yt_ps")
        self.s_yt = done("yt")
        self.s_sc_ps = done("sc_ps")
        self.s_sc = done("sc")
        self.s_alpha = done("alpha")
        self.s_heads_ps = done("heads_ps")
        self.s_ot = done("ot")
        self.s_ott_ps = done("ott_ps")
        self.s_x2 = done("x2")
        self.s_h2t_ps = done("h2t_ps")
        self.s_ht = done("ht")
        self.s_hth = done("hth")
        self.s_htl = done("htl")
        self.s_agg_ps = done("agg_ps")
        self.s_agh = done("agh")
        self.s_agl = done("agl")
        self.s_n_ps = done("n_ps")
        self.s_r_ps = done("r_ps")
        self.s_z_ps = done("z_ps")
        self.s_in_ps = done("in_ps")
        self.s_r = done("r")
        self.s_zg = done("zg")
        self.s_omz = done("omz")
        self.s_zh = done("zh")
        self.s_t = done("t")
        self.s_u = done("u")
        self.s_ng = done("ng")
        self.s_q = done("q")
        self.s_hn_ps = done("hn_ps")
        self.s_hn = done("hn")
        self.s_x3 = done("x3")
        self.s_x3b = done("x3b")
        self.s_cv_ps = done("cv_ps")
        self.s_cv = done("cv")
        self.s_out_ps = done("out_ps")
        self.s_out = done("out")


def build(nc, x, adj, mask, mask_t, w0, w1, b1, c1, w2t, wiht, whht, bih, bhh, w3, b3, cap_dram, out):
    ctx = ExitStack()
    with ctx:
        def sb(name, shape, dt=F32):
            return ctx.enter_context(nc.sbuf_tensor(name, shape, dt))

        def psum(name, shape, dt):
            return ctx.enter_context(nc.psum_tensor(name, shape, dt))

        def sem(name):
            return ctx.enter_context(nc.semaphore(name))

        W0 = sb("W0", [128, FEAT])
        W1 = sb("W1", [128, TILES, 128])
        B1 = sb("B1", [128, TILES])
        C1 = sb("C1", [128, TILES, 128])
        BIH = sb("BIH", [128, 3])
        BHH = sb("BHH", [128, 3])
        BRZ = sb("BRZ", [128, 3])
        VH = sb("VH", [128, LAYERS, 3, FEAT], F32R)
        VL = sb("VL", [128, LAYERS, 3, FEAT], F32R)
        WHHH = sb("WHHH", [128, 3, FEAT], F32R)
        WHHL = sb("WHHL", [128, 3, FEAT], F32R)
        W3 = sb("W3", [128, FEAT])
        B3 = sb("B3", [128, FEAT])
        MASKT = sb("MASKT", [128, GRAPHS])
        IDENT = sb("IDENT", [128, 128])
        MINUS_HALF = sb("MINUS_HALF", [128, GROUP])
        EPSILON = sb("EPSILON", [128, GROUP])
        ZEROS = sb("ZEROS", [128, GROUP])

        s_weights = sem("s_weights")
        s_masks = sem("s_masks")
        s_zero = sem("s_zero")
        s_ident = sem("s_ident")
        s_half = sem("s_half")
        s_mask01 = sem("s_mask01")
        s_caps = sem("s_caps")
        s_caps_out = sem("s_caps_out")
        s_maskt = sem("s_maskt")
        s_brz = sem("s_brz")
        s_v_ps = sem("s_v_ps")
        s_vh = sem("s_vh")
        s_vl = sem("s_vl")
        s_whhh = sem("s_whhh")
        s_whhl = sem("s_whhl")

        slots = [Slot(n, sb, psum, sem) for n in range(SLOTS)]
        first, second = slots

        ZERO = first.Q[:, 0, :]
        MASK = first.U[:, 0, :].bitcast(I32)
        MASK01 = first.U[:, 1, :]
        CAPS = first.U[:, 2, :]
        MASKT_I = first.U[:, 3, :].bitcast(I32)
        WIHT = first.SC[:, 0, :, :, :].rearrange("p a b n -> p (a b n)")[:, 0:3 * FEAT]
        WHHT = first.SC[:, 1, :, :, :].rearrange("p a b n -> p (a b) n")[:, 0:3, :]
        W2T = second.SC[:, 0:2, :, :, :].rearrange("p q a b n -> p (q a b) n")[:, 0:LAYERS, :]

        def after(eng, semaphore, n):
            if not isinstance(n, int) or n > 0:
                eng.wait_ge(semaphore, n)

        def at(stage, S, i, *part):
            if not isinstance(i, int) or 0 <= i < ROUNDS:
                stage(S, i, *part)

        def pipeline(eng, one_round):
            for n in range(LAG + 1):
                one_round(n)
            with eng.Fori(LAG + 1, ROUNDS) as n:
                one_round(n)
            for n in range(ROUNDS, ROUNDS + LAG):
                one_round(n)

        N_WEIGHTS = 16 * 11

        STAT_STEPS = 2 * GROUP + 1
        SCALE_STEPS = 4

        def norm_sems(S, i, norm):
            if norm == 0:
                return S.s_rows_x, S.s_scale_x, i
            return S.s_rows, S.s_scale, (NORMS - 1) * i + norm - 1

        block = ctx.enter_context(nc.Block())

        @block.sync
        def _(sp):
            def load(S, i):
                g = i * (SLOTS * GROUP) + S.n * GROUP
                after(sp, S.s_x1, i * GROUP)
                sp.dma_start(S.XIN[:, :, :],
                             x[bass.ds(g, GROUP), :, :].rearrange("b n d -> n b d"))\
                    .then_inc(S.s_x_in, 16)
                after(sp, S.s_z_raw, i)
                after(sp, S.s_a01, i)
                after(sp, S.s_adjt_ps, i)
                sp.dma_start(S.ADJ[:, :, :],
                             adj[bass.ds(g, GROUP), :, :].rearrange("b n d -> n b d"))\
                    .then_inc(S.s_adj_in, 16)

            def load_cap(S, i):
                g = i * (SLOTS * GROUP) + S.n * GROUP
                after(sp, S.s_z, i)
                sp.dma_start(S.CAP[:, :, :],
                             cap_dram[bass.ds(g, GROUP), :].partition_broadcast(128))\
                    .then_inc(S.s_cap_in, 16)

            def store(S, i):
                g = i * (SLOTS * GROUP) + S.n * GROUP
                sp.wait_ge(S.s_out, i + 1)
                sp.dma_start(out[bass.ds(g, GROUP), :, :].rearrange("b n d -> n b d"),
                             S.OUT[:, :, :]).then_inc(S.s_out_done, 16)

            load(first, 0)
            sp.dma_start(MASK, mask).then_inc(s_masks, 16)
            sp.dma_start(MASKT_I, mask_t).then_inc(s_masks, 16)
            for dst, src in [(W0[:, :], w0), (W1[:, :, :], w1), (B1[:, :], b1), (C1[:, :, :], c1),
                             (WHHT, whht), (WIHT, wiht), (W2T, w2t), (BIH[:, :], bih),
                             (BHH[:, :], bhh), (W3[:, :], w3), (B3[:, :], b3.partition_broadcast(128))]:
                sp.dma_start(dst, src).then_inc(s_weights, 16)
            load(second, 0)
            sp.wait_ge(s_caps, 1)
            sp.dma_start(cap_dram[:, :], CAPS).then_inc(s_caps_out, 16)
            sp.wait_ge(s_caps_out, 16)
            for S in slots:
                load_cap(S, 0)
            for S in slots:
                load(S, 1)
                load_cap(S, 1)
            with sp.Fori(2, ROUNDS) as i:
                for S in slots:
                    load(S, i)
                    load_cap(S, i)
                    store(S, i - 2)
            for i in (ROUNDS - 2, ROUNDS - 1):
                for S in slots:
                    store(S, i)
            for S in slots:
                sp.wait_ge(S.s_out_done, 16 * ROUNDS)

        @block.tensor
        def _(pe):
            pe.wait_ge(s_weights, N_WEIGHTS)
            for l in range(LAYERS):
                bank = (second.P + first.P[3:])[l].rearrange("p b n -> p (b n)")
                pe.matmul(bank[:, 0:3 * FEAT], W2T[:, l, :], WIHT, start=True, stop=True)\
                    .then_inc(s_v_ps, 1)
            pe.wait_ge(s_ident, 1)
            pe.wait_ge(s_vl, LAYERS)
            pe.wait_ge(s_whhl, 1)

            def turn(bank, src):
                for b in range(GROUP):
                    last = pe.transpose(bank[:, b, :], src[:, b, :], IDENT[:, :])
                return last


            def turn_ha(S, i, norm):
                pe.wait_ge(S.s_ha, GROUP * (2 * i + norm + 1))
                if norm == 0:
                    after(pe, S.s_zg, LAYERS * i)
                turn(S.P[3], S.HA).then_inc(S.s_hat_ps, 1)

            def inter(S, i):
                pe.wait_ge(S.s_hat, 2 * i + 1)
                after(pe, S.s_r, LAYERS * i)
                pe.matmul(S.P[2][:, :, :], W0[:, :], S.HAT[:, :, :], start=True, stop=True)\
                    .then_inc(S.s_it_ps, 1)

            def similarities(S, i):
                pe.wait_ge(S.s_it, i + 1)
                after(pe, S.s_x3, GROUP * i)
                for b in range(GROUP):
                    last = pe.matmul(S.P[0][:, b, :], S.IT[:, b, :], S.HAT[:, b, :],
                                     start=True, stop=True)
                last.then_inc(S.s_sim_ps, 1)

            def turn_e(S, i):
                pe.wait_ge(S.s_e, GROUP * (i + 1))
                turn(S.P[3], S.E).then_inc(S.s_et_ps, 1)

            def attend(S, i):
                pe.wait_ge(S.s_et, i + 1)
                for b in range(GROUP):
                    last = pe.matmul(S.P[0][:, b, :], S.ET[:, b, :], S.HA[:, b, :],
                                     start=True, stop=True)
                last.then_inc(S.s_att_ps, 1)

            def turn_adj(S, i):
                pe.wait_ge(S.s_adj_in, 16 * (i + 1))
                after(pe, S.s_cv, i)
                turn(S.P[1], S.ADJ).then_inc(S.s_adjt_ps, 1)

            def head_features(S, i, t):
                if t == 0:
                    pe.wait_ge(S.s_hat, 2 * i + 2)
                    pe.wait_ge(S.s_adjt, i + 1)
                    after(pe, S.s_out, i)
                pe.matmul(S.P[1 + t][:, :, :], W1[:, t, :], S.HAT[:, :, :],
                          start=True, stop=True).then_inc(S.s_xt_ps, 1)

            def head_features_c(S, i, t):
                pe.wait_ge(S.s_xt, TILES * (i + 1))
                pe.matmul(S.P[1 + t][:, :, :], C1[:, t, :], S.XT[:, t, :, :],
                          start=True, stop=True).then_inc(S.s_yt_ps, 1)

            def turn_head_features(S, i):
                pe.wait_ge(S.s_xt, TILES * (i + 1))
                for t, bank in ((0, S.P[0]), (1, S.P[3])):
                    for b in range(GROUP):
                        last = pe.transpose(bank[:, b, :], S.XT[:, t, b, :], IDENT[:, :])
                    last.then_inc(S.s_xn_ps, 1)

            def scores(S, i, k, b, t):
                if (b, t) == (0, 0):
                    pe.wait_ge(S.s_yt, TILES * (i + 1))
                    pe.wait_ge(S.s_xn, TILES * (i + 1))
                    if k:
                        pe.wait_ge(S.s_ot, 2 * i + 1)
                        pe.wait_ge(S.s_sc, QUADS * (2 * i + 1))
                for q in range(QUADS):
                    rows = slice(PAD * q, PAD * q + HEAD)
                    last = pe.matmul(S.P[q][:, TILES * b + t, :], S.XT[rows, t, HALF * k + b, :],
                                     S.YT[rows, t, HALF * k + b, :], start=True, stop=True)
                last.then_inc(S.s_sc_ps, 1)

            def heads(S, i, k):
                pe.wait_ge(S.s_alpha, QUADS * (2 * i + k + 1))
                for b in range(HALF):
                    for t in range(TILES):
                        for q in range(QUADS):
                            rows = slice(PAD * q, PAD * q + PAD)
                            last = pe.matmul(S.P[0][rows, HALF * t + b, :],
                                             S.XN[:, t, HALF * k + b, rows],
                                             S.SC[:, q, b, t, :], start=True, stop=True)
                last.then_inc(S.s_heads_ps, 1)

            def turn_heads(S, i, k):
                pe.wait_ge(S.s_ot, 2 * i + k + 1)
                if k == 0:
                    pe.wait_ge(S.s_sc, QUADS * (2 * i + 2))
                for b in range(HALF):
                    for t in range(TILES):
                        last = pe.transpose(S.P[1 + k][:, TILES * b + t, :],
                                            S.OT[:, t, HALF * k + b, :], IDENT[:, :])
                last.then_inc(S.s_ott_ps, 1)


            def turn_h2(S, i):
                pe.wait_ge(S.s_h, GROUP * (2 * i + 1))
                turn(S.P[0], S.H).then_inc(S.s_h2t_ps, 1)

            def hidden(bank, c, S):
                pe.matmul(bank[:, :, :], WHHH[:, c, :], S.HTH[:, :, :], start=True, stop=False)
                pe.matmul(bank[:, :, :], WHHL[:, c, :], S.HTH[:, :, :], start=False, stop=False)

            def gates_hidden(S, i, l):
                pe.wait_ge(S.s_hth, LAYERS * i + l + 1)
                hidden(S.P[2], 0, S)
                hidden(S.P[3], 1, S)

            def aggregate(S, i, l):
                if l == 0:
                    pe.wait_ge(S.s_a01, i + 1)
                    pe.wait_ge(S.s_ht, (LAYERS + 1) * i + 1)
                else:
                    pe.wait_ge(S.s_hn, (LAYERS - 1) * i + l)
                for b in range(GROUP):
                    last = pe.matmul(S.P[0][:, b, :], S.H[:, b, :], S.A01[:, b, :],
                                     start=True, stop=True)
                last.then_inc(S.s_agg_ps, 1)

            def gates_low(S, i, l):
                hidden(S.P[1], 2, S)
                pe.wait_ge(S.s_htl, LAYERS * i + l + 1)
                pe.matmul(S.P[1][:, :, :], WHHH[:, 2, :], S.HTL[:, :, :], start=False, stop=True)\
                    .then_inc(S.s_n_ps, 1)
                pe.matmul(S.P[2][:, :, :], WHHH[:, 0, :], S.HTL[:, :, :], start=False, stop=False)
                pe.matmul(S.P[3][:, :, :], WHHH[:, 1, :], S.HTL[:, :, :], start=False, stop=False)

            def gates_input(S, i, l):
                pe.wait_ge(S.s_agh, LAYERS * i + l + 1)
                for c in (0, 1):
                    bank = S.P[2 + c]
                    pe.matmul(bank[:, :, :], VH[:, l, c, :], S.AGH[:, :, :], start=False, stop=False)
                    pe.matmul(bank[:, :, :], VL[:, l, c, :], S.AGH[:, :, :], start=False, stop=False)
                pe.wait_ge(S.s_agl, LAYERS * i + l + 1)
                pe.matmul(S.P[2][:, :, :], VH[:, l, 0, :], S.AGL[:, :, :], start=False, stop=True)\
                    .then_inc(S.s_r_ps, 1)
                pe.matmul(S.P[3][:, :, :], VH[:, l, 1, :], S.AGL[:, :, :], start=False, stop=True)\
                    .then_inc(S.s_z_ps, 1)
                pe.matmul(S.P[0][:, :, :], VH[:, l, 2, :], S.AGH[:, :, :], start=True, stop=False)
                pe.matmul(S.P[0][:, :, :], VL[:, l, 2, :], S.AGH[:, :, :], start=False, stop=False)
                pe.matmul(S.P[0][:, :, :], VH[:, l, 2, :], S.AGL[:, :, :], start=False, stop=True)\
                    .then_inc(S.s_in_ps, 1)

            def turn_new(S, i, l):
                pe.wait_ge(S.s_ht, (LAYERS + 1) * i + l + 2)
                turn(S.P[0], S.HT).then_inc(S.s_hn_ps, 1)


            def conv(S, i):
                pe.wait_ge(S.s_h, GROUP * (2 * i + 2))
                for b in range(GROUP):
                    last = pe.matmul(S.P[1][:, b, :], S.H[:, b, :], S.ADJT[:, b, :],
                                     start=True, stop=True)
                last.then_inc(S.s_cv_ps, 1)

            def conv_out(S, i):
                pe.wait_ge(S.s_cv, i + 1)
                if not isinstance(i, int) or i + 1 < ROUNDS:
                    pe.wait_ge(S.s_it, i + 2)
                for b in range(GROUP):
                    last = pe.matmul(S.P[2][:, b, :], S.CV[:, b, :], W3[:, :],
                                     start=True, stop=True)
                last.then_inc(S.s_out_ps, 1)

            def one_round(n):
                at(turn_head_features, first, n - 1)
                at(head_features_c, first, n - 1, 1)
                at(turn_head_features, second, n - 1)
                at(head_features_c, second, n - 1, 0)
                at(scores, first, n - 1, 0, 0, 0)
                at(scores, first, n - 1, 0, 0, 1)
                at(head_features_c, second, n - 1, 1)
                at(scores, first, n - 1, 0, 1, 0)
                at(scores, first, n - 1, 0, 1, 1)
                at(scores, second, n - 1, 0, 0, 0)
                at(scores, second, n - 1, 0, 0, 1)
                at(scores, second, n - 1, 0, 1, 0)
                at(heads, first, n - 1, 0)
                at(scores, second, n - 1, 0, 1, 1)
                at(scores, first, n - 1, 1, 0, 0)
                at(scores, first, n - 1, 1, 0, 1)
                at(scores, first, n - 1, 1, 1, 0)
                at(heads, second, n - 1, 0)
                at(scores, first, n - 1, 1, 1, 1)
                at(scores, second, n - 1, 1, 0, 0)
                at(scores, second, n - 1, 1, 0, 1)
                at(scores, second, n - 1, 1, 1, 0)
                at(scores, second, n - 1, 1, 1, 1)
                at(heads, first, n - 1, 1)
                at(turn_heads, first, n - 1, 0)
                at(turn_heads, first, n - 1, 1)
                at(heads, second, n - 1, 1)
                at(turn_heads, second, n - 1, 0)
                at(turn_heads, second, n - 1, 1)
                at(turn_h2, first, n - 1)
                at(gates_hidden, first, n - 1, 0)
                at(aggregate, first, n - 1, 0)
                at(gates_low, first, n - 1, 0)
                at(turn_h2, second, n - 1)
                at(gates_input, first, n - 1, 0)
                at(gates_hidden, second, n - 1, 0)
                at(aggregate, second, n - 1, 0)
                at(gates_low, second, n - 1, 0)
                at(gates_input, second, n - 1, 0)
                at(turn_new, first, n - 1, 0)
                at(gates_hidden, first, n - 1, 1)
                at(aggregate, first, n - 1, 1)
                at(gates_low, first, n - 1, 1)
                at(gates_input, first, n - 1, 1)
                at(turn_new, second, n - 1, 0)
                at(gates_hidden, second, n - 1, 1)
                at(aggregate, second, n - 1, 1)
                at(gates_low, second, n - 1, 1)
                at(gates_input, second, n - 1, 1)
                at(turn_new, first, n - 1, 1)
                at(gates_hidden, first, n - 1, 2)
                at(aggregate, first, n - 1, 2)
                at(gates_low, first, n - 1, 2)
                at(gates_input, first, n - 1, 2)
                at(turn_new, second, n - 1, 1)
                at(gates_hidden, second, n - 1, 2)
                at(aggregate, second, n - 1, 2)
                at(gates_low, second, n - 1, 2)
                at(gates_input, second, n - 1, 2)
                at(turn_new, first, n - 1, 2)
                at(gates_hidden, first, n - 1, 3)
                at(aggregate, first, n - 1, 3)
                at(gates_low, first, n - 1, 3)
                at(gates_input, first, n - 1, 3)
                at(turn_new, second, n - 1, 2)
                at(gates_hidden, second, n - 1, 3)
                at(aggregate, second, n - 1, 3)
                at(gates_low, second, n - 1, 3)
                at(gates_input, second, n - 1, 3)
                at(turn_new, first, n - 1, 3)
                at(gates_hidden, first, n - 1, 4)
                at(aggregate, first, n - 1, 4)
                at(gates_low, first, n - 1, 4)
                at(gates_input, first, n - 1, 4)
                at(turn_new, second, n - 1, 3)
                at(gates_hidden, second, n - 1, 4)
                at(aggregate, second, n - 1, 4)
                at(gates_low, second, n - 1, 4)
                at(gates_input, second, n - 1, 4)
                at(turn_ha, first, n, 0)
                at(turn_new, first, n - 1, 4)
                at(turn_ha, second, n, 0)
                at(inter, second, n)
                at(inter, first, n)
                at(turn_new, second, n - 1, 4)
                at(similarities, first, n)
                at(conv, first, n - 1)
                at(similarities, second, n)
                at(turn_e, first, n)
                at(attend, first, n)
                at(conv, second, n - 1)
                at(turn_e, second, n)
                at(attend, second, n)
                at(turn_adj, first, n)
                at(conv_out, first, n - 1)
                at(turn_adj, second, n)
                at(turn_ha, first, n, 1)
                at(conv_out, second, n - 1)
                at(head_features, first, n, 0)
                at(head_features, first, n, 1)
                at(turn_ha, second, n, 1)
                at(head_features, second, n, 0)
                at(head_features, second, n, 1)
                at(head_features_c, first, n, 0)

            pipeline(pe, one_round)

        @block.scalar
        def _(act):
            act.wait_ge(s_weights, N_WEIGHTS)
            act.wait_ge(s_brz, 1)

            def normed(S, i, norm, k):
                src = (S.XIN, S.X1, S.X2, S.X3)[norm]
                dst, done = ((S.HA, S.s_ha), (S.HA, S.s_ha), (S.H, S.s_h), (S.H, S.s_h))[norm]
                if k == 0:
                    scaled, before = norm_sems(S, i, norm)[1:]
                    act.wait_ge(scaled, SCALE_STEPS * (before + 1))
                    if norm == 0:
                        after(act, S.s_att_ps, i)
                        after(act, S.s_hat_ps, 2 * i)
                    elif norm == 2:
                        after(act, S.s_cv_ps, i)
                for b in range(HALF * k, HALF * k + HALF):
                    act.activation(dst[:, b, :], src[:, b, :], ACT.Relu,
                                   bias=S.SHIFT[:, norm, b:b + 1], scale=S.RSTD[:, norm, b:b + 1])\
                        .then_inc(done, 1)

            def adj_t(S, i):
                act.wait_ge(S.s_adjt_ps, i + 1)
                act.copy(S.ADJT[:, :, :], S.P[1][:, :, :]).then_inc(S.s_adjt, 1)

            def ha_t(S, i, norm):
                act.wait_ge(S.s_hat_ps, 2 * i + norm + 1)
                act.copy(S.HAT[:, :, :], S.P[3][:, :, :]).then_inc(S.s_hat, 1)

            def exps(S, i, k):
                act.wait_ge(S.s_nmax, i + 1)
                for b in range(HALF * k, HALF * k + HALF):
                    act.activation(S.E[:, b, :], S.Z[:, b, :], ACT.Exp,
                                   bias=S.NMAX[:, b:b + 1], accum_out=S.SUM[:, b:b + 1])\
                        .then_inc(S.s_e, 1)

            def e_t(S, i):
                act.wait_ge(S.s_et_ps, i + 1)
                act.copy(S.ET[:, :, :], S.P[3][:, :, :]).then_inc(S.s_et, 1)

            def features(S, i):
                for t in range(TILES):
                    act.wait_ge(S.s_xt_ps, TILES * i + t + 1)
                    act.activation(S.XT[:, t, :, :], S.P[1 + t][:, :, :], ACT.Identity,
                                   bias=B1[:, t:t + 1]).then_inc(S.s_xt, 1)

            def features_c(S, i):
                for t in range(TILES):
                    act.wait_ge(S.s_yt_ps, TILES * i + t + 1)
                    act.copy(S.YT[:, t, :, :], S.P[1 + t][:, :, :]).then_inc(S.s_yt, 1)

            def features_natural(S, i):
                for t, bank in ((0, S.P[0]), (1, S.P[3])):
                    act.wait_ge(S.s_xn_ps, TILES * i + t + 1)
                    act.copy(S.XN[:, t, :, :], bank[:, :, :]).then_inc(S.s_xn, 1)

            def alphas(S, i, k, q):
                act.wait_ge(S.s_sc, QUADS * (2 * i + k) + q + 1)
                act.activation(S.SC[:, q, :, :, :], S.SC[:, q, :, :, :], ACT.Tanh)\
                    .then_inc(S.s_alpha, 1)

            def h_t(S, i):
                act.wait_ge(S.s_h2t_ps, i + 1)
                act.copy(S.HTH[:, :, :], S.P[0][:, :, :]).then_inc(S.s_hth, 1)
                act.copy(S.HT[:, :, :], S.P[0][:, :, :]).then_inc(S.s_ht, 1)

            def aggregated(S, i, l):
                act.wait_ge(S.s_agg_ps, LAYERS * i + l + 1)
                act.copy(S.AGH[:, :, :], S.P[0][:, :, :]).then_inc(S.s_agh, 1)

            def gates(S, i, l):
                act.wait_ge(S.s_r_ps, LAYERS * i + l + 1)
                act.activation(S.R[:, :, :], S.P[2][:, :, :], ACT.Sigmoid, bias=BRZ[:, 0:1])\
                    .then_inc(S.s_r, 1)
                act.wait_ge(S.s_z_ps, LAYERS * i + l + 1)
                act.activation(S.ZG[:, :, :], S.P[3][:, :, :], ACT.Sigmoid, bias=BRZ[:, 1:2])\
                    .then_inc(S.s_zg, 1)

            def gate_n(S, i, l):
                act.wait_ge(S.s_u, LAYERS * i + l + 1)
                act.activation(S.NG[:, :, :], S.U[:, :, :], ACT.Tanh, bias=BIH[:, 2:3])\
                    .then_inc(S.s_ng, 1)

            def h_natural(S, i, l):
                act.wait_ge(S.s_hn_ps, LAYERS * i + l + 1)
                act.copy(S.H[:, :, :], S.P[0][:, :, :]).then_inc(S.s_hn, 1)

            def conved(S, i):
                act.wait_ge(S.s_cv_ps, i + 1)
                act.copy(S.CV[:, :, :], S.P[1][:, :, :]).then_inc(S.s_cv, 1)

            def one_round(n):
                at(ha_t, second, n - 1, 1)
                at(features, first, n - 1)
                at(features, second, n - 1)
                at(features_natural, first, n - 1)
                at(features_c, first, n - 1)
                at(features_c, second, n - 1)
                at(features_natural, second, n - 1)
                at(alphas, first, n - 1, 0, 0)
                at(alphas, first, n - 1, 0, 1)
                at(alphas, first, n - 1, 0, 2)
                at(alphas, first, n - 1, 0, 3)
                at(alphas, second, n - 1, 0, 0)
                at(alphas, second, n - 1, 0, 1)
                at(alphas, second, n - 1, 0, 2)
                at(alphas, second, n - 1, 0, 3)
                at(alphas, first, n - 1, 1, 0)
                at(alphas, first, n - 1, 1, 2)
                at(alphas, first, n - 1, 1, 3)
                at(alphas, first, n - 1, 1, 1)
                at(alphas, second, n - 1, 1, 0)
                at(alphas, second, n - 1, 1, 2)
                at(alphas, second, n - 1, 1, 1)
                at(alphas, second, n - 1, 1, 3)
                at(normed, first, n - 1, 2, 0)
                at(normed, first, n - 1, 2, 1)
                at(h_t, first, n - 1)
                at(normed, second, n - 1, 2, 0)
                at(normed, second, n - 1, 2, 1)
                at(aggregated, first, n - 1, 0)
                at(h_t, second, n - 1)
                at(gates, first, n - 1, 0)
                at(gate_n, first, n - 1, 0)
                at(aggregated, second, n - 1, 0)
                at(gates, second, n - 1, 0)
                at(h_natural, first, n - 1, 0)
                at(gate_n, second, n - 1, 0)
                at(aggregated, first, n - 1, 1)
                at(gates, first, n - 1, 1)
                at(h_natural, second, n - 1, 0)
                at(gate_n, first, n - 1, 1)
                at(aggregated, second, n - 1, 1)
                at(normed, first, n, 0, 0)
                at(gates, second, n - 1, 1)
                at(h_natural, first, n - 1, 1)
                at(gate_n, second, n - 1, 1)
                at(aggregated, first, n - 1, 2)
                at(gates, first, n - 1, 2)
                at(h_natural, second, n - 1, 1)
                at(gate_n, first, n - 1, 2)
                at(aggregated, second, n - 1, 2)
                at(gates, second, n - 1, 2)
                at(h_natural, first, n - 1, 2)
                at(gate_n, second, n - 1, 2)
                at(aggregated, first, n - 1, 3)
                at(gates, first, n - 1, 3)
                at(h_natural, second, n - 1, 2)
                at(gate_n, first, n - 1, 3)
                at(aggregated, second, n - 1, 3)
                at(gates, second, n - 1, 3)
                at(h_natural, first, n - 1, 3)
                at(gate_n, second, n - 1, 3)
                at(aggregated, first, n - 1, 4)
                at(normed, second, n, 0, 0)
                at(gates, first, n - 1, 4)
                at(h_natural, second, n - 1, 3)
                at(normed, first, n, 0, 1)
                at(gate_n, first, n - 1, 4)
                at(aggregated, second, n - 1, 4)
                at(normed, second, n, 0, 1)
                at(gates, second, n - 1, 4)
                at(ha_t, first, n, 0)
                at(ha_t, second, n, 0)
                at(gate_n, second, n - 1, 4)
                at(normed, first, n - 1, 3, 0)
                at(normed, first, n - 1, 3, 1)
                at(normed, second, n - 1, 3, 0)
                at(exps, first, n, 0)
                at(exps, first, n, 1)
                at(normed, second, n - 1, 3, 1)
                at(e_t, first, n)
                at(exps, second, n, 0)
                at(exps, second, n, 1)
                at(conved, first, n - 1)
                at(e_t, second, n)
                at(conved, second, n - 1)
                at(normed, first, n, 1, 0)
                at(normed, first, n, 1, 1)
                at(adj_t, first, n)
                at(ha_t, first, n, 1)
                at(adj_t, second, n)
                at(normed, second, n, 1, 0)
                at(normed, second, n, 1, 1)

            pipeline(act, one_round)

        @block.gpsimd
        def _(pool):
            pool.memset(ZERO, 0.0).then_inc(s_zero, 1)
            pool.memset(MINUS_HALF[:, :], -0.5).then_inc(s_half, 1)
            pool.memset(EPSILON[:, :], EPS).then_inc(s_half, 1)
            pool.memset(ZEROS[:, :], 0.0).then_inc(s_half, 1)
            pool.wait_ge(s_zero, 1)
            pool.affine_select(out=IDENT[:, :], in_=ZERO, compare_op=ALU.not_equal, fill=1.0,
                               base=0, pattern=[[-1, 128]], channel_multiplier=1)\
                .then_inc(s_ident, 1)
            pool.wait_ge(s_half, 3)
            pool.wait_ge(s_weights, N_WEIGHTS)
            pool.wait_ge(s_ident, 1)

            def scales(S, i, norm):
                rows, scaled, before = norm_sems(S, i, norm)
                pool.wait_ge(rows, STAT_STEPS * (before + 1))
                pool.tensor_tensor(S.VE[:, norm, :], S.MV[:, norm, :, 1], EPSILON[:, :], ALU.add)\
                    .then_inc(scaled, 1)
                pool.tensor_tensor(S.NMEAN[:, norm, :], ZEROS[:, :], S.MV[:, norm, :, 0],
                                   ALU.subtract).then_inc(scaled, 1)
                pool.wait_ge(scaled, SCALE_STEPS * before + 2)
                pool.tensor_tensor(S.RSTD[:, norm, :], S.VE[:, norm, :], MINUS_HALF[:, :], ALU.pow)\
                    .then_inc(scaled, 1)
                pool.wait_ge(scaled, SCALE_STEPS * before + 3)
                pool.tensor_tensor(S.SHIFT[:, norm, :], S.NMEAN[:, norm, :], S.RSTD[:, norm, :],
                                   ALU.mult).then_inc(scaled, 1)

            def h_low(S, i, l):
                pool.wait_ge(S.s_ht, (LAYERS + 1) * i + l + 1)
                pool.wait_ge(S.s_hth, LAYERS * i + l + 1)
                pool.tensor_tensor(S.HTL[:, :, :], S.HT[:, :, :], S.HTH[:, :, :].bitcast(F32),
                                   ALU.subtract).then_inc(S.s_htl, 1)

            def mix(S, i, l):
                pool.wait_ge(S.s_zg, LAYERS * i + l + 1)
                pool.tensor_tensor(S.ZH[:, :, :], S.ZG[:, :, :], S.HT[:, :, :], ALU.mult)\
                    .then_inc(S.s_zh, 1)

            def bias_out(S, i):
                pool.wait_ge(S.s_x3, GROUP * (i + 1))
                pool.tensor_tensor(S.X3B[:, :, :], S.X3[:, :, :],
                                   B3[:, :].unsqueeze(1).to_broadcast([128, GROUP, FEAT]),
                                   ALU.add).then_inc(S.s_x3b, 1)

            def one_round(n):
                at(bias_out, first, n - 2)
                at(scales, second, n - 1, 1)
                at(scales, first, n - 1, 2)
                at(scales, first, n, 0)
                at(scales, second, n - 1, 2)
                at(h_low, first, n - 1, 0)
                at(h_low, second, n - 1, 0)
                at(mix, first, n - 1, 0)
                at(h_low, first, n - 1, 1)
                at(mix, second, n - 1, 0)
                at(h_low, second, n - 1, 1)
                at(mix, first, n - 1, 1)
                at(h_low, first, n - 1, 2)
                at(scales, second, n, 0)
                at(mix, second, n - 1, 1)
                at(h_low, second, n - 1, 2)
                at(mix, first, n - 1, 2)
                at(h_low, first, n - 1, 3)
                at(mix, second, n - 1, 2)
                at(h_low, second, n - 1, 3)
                at(mix, first, n - 1, 3)
                at(h_low, first, n - 1, 4)
                at(mix, second, n - 1, 3)
                at(h_low, second, n - 1, 4)
                at(mix, first, n - 1, 4)
                at(mix, second, n - 1, 4)
                at(scales, first, n - 1, 3)
                at(scales, second, n - 1, 3)
                at(bias_out, second, n - 1)
                at(scales, first, n, 1)

            pipeline(pool, one_round)

        @block.vector
        def _(dve):
            dve.wait_ge(s_masks, 32)
            dve.tensor_scalar(MASK01, MASK, 0.0, None, ALU.not_equal).then_inc(s_mask01, 1)
            dve.tensor_copy(MASKT[:, :], MASKT_I).then_inc(s_maskt, 1)
            dve.wait_ge(s_mask01, 1)
            dve.tensor_scalar(CAPS, MASK01, TOP, NEG, ALU.mult, ALU.add).then_inc(s_caps, 1)
            dve.wait_ge(s_weights, N_WEIGHTS)
            dve.tensor_tensor(BRZ[:, :], BIH[:, :], BHH[:, :], ALU.add).then_inc(s_brz, 1)
            dve.tensor_copy(WHHH[:, :, :], WHHT).then_inc(s_whhh, 1)
            dve.wait_ge(s_whhh, 1)
            dve.tensor_tensor(WHHL[:, :, :], WHHT, WHHH[:, :, :].bitcast(F32), ALU.subtract)\
                .then_inc(s_whhl, 1)
            for l in range(LAYERS):
                dve.wait_ge(s_v_ps, l + 1)
                bank = (second.P + first.P[3:])[l]
                dve.tensor_copy(VH[:, l, :, :], bank[:, 0:3, :]).then_inc(s_vh, 1)
                dve.wait_ge(s_vh, l + 1)
                dve.tensor_tensor(VL[:, l, :, :], bank[:, 0:3, :], VH[:, l, :, :].bitcast(F32),
                                  ALU.subtract).then_inc(s_vl, 1)
            dve.wait_ge(s_maskt, 1)
            dve.wait_ge(s_whhl, 1)
            dve.wait_ge(s_caps_out, 16)

            def stats(S, i, norm, k):
                src = (S.XIN, S.X1, S.X2, S.X3)[norm]
                rows = norm_sems(S, i, norm)[0]
                if norm == 0:
                    dve.wait_ge(S.s_x_in, 16 * (i + 1))
                elif norm == 1:
                    dve.wait_ge(S.s_x1, GROUP * (i + 1))
                elif norm == 2:
                    dve.wait_ge(S.s_x2, 2 * (i + 1))
                else:
                    dve.wait_ge(S.s_x3, GROUP * (i + 1))
                for b in range(HALF * k, HALF * k + HALF):
                    dve.bn_stats(S.STAT[:, norm, b, :], src[:, b, :]).then_inc(rows, 1)

            def means(S, i, norm):
                rows, _, before = norm_sems(S, i, norm)
                dve.wait_ge(rows, STAT_STEPS * before + GROUP)
                dve.tensor_copy(S.COUNT[:, norm, :], S.STAT[:, norm, :, 0]).then_inc(rows, 1)
                for b in range(GROUP):
                    dve.bn_aggr(S.MV[:, norm, b, :], S.STAT[:, norm, b, :]).then_inc(rows, 1)

            def adj_nonzero(S, i):
                dve.wait_ge(S.s_adj_in, 16 * (i + 1))
                dve.tensor_scalar(S.A01[:, :, :], S.ADJ[:, :, :], 0.0, None, ALU.not_equal)\
                    .then_inc(S.s_a01, 1)

            def inter(S, i):
                dve.wait_ge(S.s_it_ps, i + 1)
                dve.tensor_copy(S.IT[:, :, :], S.P[2][:, :, :]).then_inc(S.s_it, 1)

            def times_adj(S, i):
                dve.wait_ge(S.s_sim_ps, i + 1)
                dve.wait_ge(S.s_adj_in, 16 * (i + 1))
                dve.tensor_tensor(S.ZRAW[:, :, :], S.P[0][:, :, :], S.ADJ[:, :, :], ALU.mult)\
                    .then_inc(S.s_z_raw, 1)

            def capped(S, i):
                dve.wait_ge(S.s_z_raw, i + 1)
                dve.wait_ge(S.s_cap_in, 16 * (i + 1))
                dve.tensor_tensor(S.Z[:, :, :], S.ZRAW[:, :, :], S.CAP[:, :, :], ALU.min)\
                    .then_inc(S.s_z, 1)

            def maxima(S, i):
                dve.wait_ge(S.s_z, i + 1)
                dve.tensor_reduce(S.NMAX[:, :], S.Z[:, :, :], X_AXIS, ALU.max, negate=True)\
                    .then_inc(S.s_nmax, 1)

            def add_attention(S, i):
                dve.wait_ge(S.s_e, GROUP * (i + 1))
                dve.reciprocal(S.RSUM[:, :], S.SUM[:, :]).then_inc(S.s_rsum, 1)
                dve.wait_ge(S.s_rsum, i + 1)
                dve.wait_ge(S.s_att_ps, i + 1)
                for b in range(GROUP):
                    dve.scalar_tensor_tensor(out=S.X1[:, b, :], in0=S.P[0][:, b, :],
                                             scalar=S.RSUM[:, b:b + 1], in1=S.XIN[:, b, :],
                                             op0=ALU.mult, op1=ALU.add).then_inc(S.s_x1, 1)

            def weigh_scores(S, i, k, q):
                dve.wait_ge(S.s_sc_ps, HALF * TILES * (2 * i + k + 1))
                both = S.ADJT[:, HALF * k:HALF * k + HALF, :].unsqueeze(2)\
                    .to_broadcast([128, HALF, TILES, 128])
                bank = S.P[q][:, :, :].rearrange("p (b t) n -> p b t n", t=TILES)
                dve.tensor_tensor(S.SC[:, q, :, :, :], bank, both, ALU.mult).then_inc(S.s_sc, 1)

            def heads_out(S, i, k):
                dve.wait_ge(S.s_heads_ps, 2 * i + k + 1)
                bank = S.P[0][:, :, :].rearrange("p (t b) n -> p t b n", b=HALF)
                dve.tensor_copy(S.OT[:, :, HALF * k:HALF * k + HALF, :], bank)\
                    .then_inc(S.s_ot, 1)

            def add_heads(S, i, k):
                dve.wait_ge(S.s_ott_ps, 2 * i + k + 1)
                graphs = slice(HALF * k, HALF * k + HALF)
                real = S.P[1 + k][:, :, :].rearrange("p (b t) (q w) -> p b (t q) w",
                                                     t=TILES, w=PAD)[:, :, :, 0:HEAD]
                dve.tensor_tensor(
                    S.X2[:, graphs, :].rearrange("p b (h w) -> p b h w", w=HEAD), real,
                    S.X1[:, graphs, :].rearrange("p b (h w) -> p b h w", w=HEAD), ALU.add)\
                    .then_inc(S.s_x2, 1)

            def aggregate_low(S, i, l):
                dve.wait_ge(S.s_agh, LAYERS * i + l + 1)
                dve.tensor_tensor(S.AGL[:, :, :], S.P[0][:, :, :], S.AGH[:, :, :].bitcast(F32),
                                  ALU.subtract).then_inc(S.s_agl, 1)

            def reset(S, i, l):
                dve.wait_ge(S.s_n_ps, LAYERS * i + l + 1)
                dve.wait_ge(S.s_r, LAYERS * i + l + 1)
                dve.scalar_tensor_tensor(out=S.T[:, :, :], in0=S.P[1][:, :, :],
                                         scalar=BHH[:, 2:3], in1=S.R[:, :, :],
                                         op0=ALU.add, op1=ALU.mult).then_inc(S.s_t, 1)

            def one_minus_z(S, i, l):
                dve.wait_ge(S.s_zg, LAYERS * i + l + 1)
                dve.tensor_scalar(S.OMZ[:, :, :], S.ZG[:, :, :], -1.0, 1.0, ALU.mult, ALU.add)\
                    .then_inc(S.s_omz, 1)

            def n_input(S, i, l):
                dve.wait_ge(S.s_t, LAYERS * i + l + 1)
                dve.wait_ge(S.s_in_ps, LAYERS * i + l + 1)
                dve.tensor_tensor(S.U[:, :, :], S.P[0][:, :, :], S.T[:, :, :], ALU.add)\
                    .then_inc(S.s_u, 1)

            def n_share(S, i, l):
                dve.wait_ge(S.s_omz, LAYERS * i + l + 1)
                dve.wait_ge(S.s_ng, LAYERS * i + l + 1)
                dve.tensor_tensor(S.Q[:, :, :], S.NG[:, :, :], S.OMZ[:, :, :], ALU.mult)\
                    .then_inc(S.s_q, 1)

            def new_high(S, i, l):
                dve.wait_ge(S.s_zh, LAYERS * i + l + 1)
                dve.wait_ge(S.s_q, LAYERS * i + l + 1)
                dve.tensor_tensor(S.HTH[:, :, :], S.Q[:, :, :], S.ZH[:, :, :], ALU.add)\
                    .then_inc(S.s_hth, 1)

            def new(S, i, l):
                dve.wait_ge(S.s_zh, LAYERS * i + l + 1)
                dve.wait_ge(S.s_q, LAYERS * i + l + 1)
                dve.tensor_tensor(S.HT[:, :, :], S.Q[:, :, :], S.ZH[:, :, :], ALU.add)\
                    .then_inc(S.s_ht, 1)

            def add_hidden(S, i):
                dve.wait_ge(S.s_hn_ps, LAYERS * (i + 1))
                for b in range(GROUP):
                    graph = i * (SLOTS * GROUP) + S.n * GROUP + b
                    dve.scalar_tensor_tensor(out=S.X3[:, b, :], in0=S.P[0][:, b, :],
                                             scalar=MASKT[:, bass.ds(graph, 1)],
                                             in1=S.X2[:, b, :],
                                             op0=ALU.mult, op1=ALU.add).then_inc(S.s_x3, 1)

            def result(S, i):
                dve.wait_ge(S.s_out_ps, i + 1)
                dve.wait_ge(S.s_x3b, i + 1)
                after(dve, S.s_out_done, 16 * i)
                dve.tensor_tensor(S.OUT[:, :, :], S.P[2][:, :, :], S.X3B[:, :, :], ALU.add)\
                    .then_inc(S.s_out, 1)

            def one_round(n):
                at(stats, first, n, 0, 0)
                at(adj_nonzero, second, n - 1)
                at(result, first, n - 2)
                at(result, second, n - 2)
                at(stats, first, n, 0, 1)
                at(weigh_scores, first, n - 1, 0, 0)
                at(weigh_scores, first, n - 1, 0, 1)
                at(weigh_scores, first, n - 1, 0, 2)
                at(weigh_scores, first, n - 1, 0, 3)
                at(heads_out, first, n - 1, 0)
                at(adj_nonzero, first, n - 1)
                at(weigh_scores, second, n - 1, 0, 0)
                at(weigh_scores, second, n - 1, 0, 1)
                at(weigh_scores, second, n - 1, 0, 2)
                at(weigh_scores, second, n - 1, 0, 3)
                at(heads_out, second, n - 1, 0)
                at(weigh_scores, first, n - 1, 1, 0)
                at(weigh_scores, first, n - 1, 1, 1)
                at(weigh_scores, first, n - 1, 1, 2)
                at(weigh_scores, first, n - 1, 1, 3)
                at(weigh_scores, second, n - 1, 1, 0)
                at(weigh_scores, second, n - 1, 1, 1)
                at(heads_out, first, n - 1, 1)
                at(weigh_scores, second, n - 1, 1, 2)
                at(add_heads, first, n - 1, 0)
                at(weigh_scores, second, n - 1, 1, 3)
                at(add_heads, first, n - 1, 1)
                at(stats, first, n - 1, 2, 0)
                at(stats, first, n - 1, 2, 1)
                at(means, first, n - 1, 2)
                at(heads_out, second, n - 1, 1)
                at(means, first, n, 0)
                at(add_heads, second, n - 1, 0)
                at(add_heads, second, n - 1, 1)
                at(stats, second, n - 1, 2, 0)
                at(stats, second, n - 1, 2, 1)
                at(means, second, n - 1, 2)
                at(stats, second, n, 0, 0)
                at(aggregate_low, first, n - 1, 0)
                at(reset, first, n - 1, 0)
                at(n_input, first, n - 1, 0)
                at(one_minus_z, first, n - 1, 0)
                at(stats, second, n, 0, 1)
                at(n_share, first, n - 1, 0)
                at(aggregate_low, second, n - 1, 0)
                at(new_high, first, n - 1, 0)
                at(new, first, n - 1, 0)
                at(reset, second, n - 1, 0)
                at(means, second, n, 0)
                at(n_input, second, n - 1, 0)
                at(one_minus_z, second, n - 1, 0)
                at(n_share, second, n - 1, 0)
                at(aggregate_low, first, n - 1, 1)
                at(new_high, second, n - 1, 0)
                at(new, second, n - 1, 0)
                at(reset, first, n - 1, 1)
                at(n_input, first, n - 1, 1)
                at(one_minus_z, first, n - 1, 1)
                at(n_share, first, n - 1, 1)
                at(new_high, first, n - 1, 1)
                at(aggregate_low, second, n - 1, 1)
                at(new, first, n - 1, 1)
                at(reset, second, n - 1, 1)
                at(n_input, second, n - 1, 1)
                at(one_minus_z, second, n - 1, 1)
                at(n_share, second, n - 1, 1)
                at(aggregate_low, first, n - 1, 2)
                at(new_high, second, n - 1, 1)
                at(new, second, n - 1, 1)
                at(reset, first, n - 1, 2)
                at(one_minus_z, first, n - 1, 2)
                at(n_input, first, n - 1, 2)
                at(n_share, first, n - 1, 2)
                at(aggregate_low, second, n - 1, 2)
                at(new_high, first, n - 1, 2)
                at(new, first, n - 1, 2)
                at(reset, second, n - 1, 2)
                at(n_input, second, n - 1, 2)
                at(one_minus_z, second, n - 1, 2)
                at(n_share, second, n - 1, 2)
                at(new_high, second, n - 1, 2)
                at(aggregate_low, first, n - 1, 3)
                at(new, second, n - 1, 2)
                at(reset, first, n - 1, 3)
                at(n_input, first, n - 1, 3)
                at(one_minus_z, first, n - 1, 3)
                at(n_share, first, n - 1, 3)
                at(new_high, first, n - 1, 3)
                at(aggregate_low, second, n - 1, 3)
                at(new, first, n - 1, 3)
                at(reset, second, n - 1, 3)
                at(one_minus_z, second, n - 1, 3)
                at(n_input, second, n - 1, 3)
                at(n_share, second, n - 1, 3)
                at(aggregate_low, first, n - 1, 4)
                at(new_high, second, n - 1, 3)
                at(new, second, n - 1, 3)
                at(reset, first, n - 1, 4)
                at(one_minus_z, first, n - 1, 4)
                at(n_input, first, n - 1, 4)
                at(aggregate_low, second, n - 1, 4)
                at(n_share, first, n - 1, 4)
                at(new, first, n - 1, 4)
                at(reset, second, n - 1, 4)
                at(one_minus_z, second, n - 1, 4)
                at(n_input, second, n - 1, 4)
                at(add_hidden, first, n - 1)
                at(n_share, second, n - 1, 4)
                at(stats, first, n - 1, 3, 0)
                at(new, second, n - 1, 4)
                at(stats, first, n - 1, 3, 1)
                at(inter, first, n)
                at(add_hidden, second, n - 1)
                at(means, first, n - 1, 3)
                at(stats, second, n - 1, 3, 0)
                at(stats, second, n - 1, 3, 1)
                at(means, second, n - 1, 3)
                at(times_adj, first, n)
                at(capped, first, n)
                at(maxima, first, n)
                at(inter, second, n)
                at(times_adj, second, n)
                at(capped, second, n)
                at(maxima, second, n)
                at(add_attention, first, n)
                at(stats, first, n, 1, 0)
                at(stats, first, n, 1, 1)
                at(means, first, n, 1)
                at(add_attention, second, n)
                at(stats, second, n, 1, 0)
                at(stats, second, n, 1, 1)
                at(means, second, n, 1)

            pipeline(dve, one_round)


def kernel(x, adj, nodemask, L0_gnn_W, L1_gnn_W, L1_gnn_b, L1_gnn_C, L2_gnn_weight, L2_gnn_w_ih,
           L2_gnn_w_hh, L2_gnn_b_ih, L2_gnn_b_hh, L3_gnn_weight, L3_gnn_bias):
    import numpy as np
    import concourse.bacc as bacc
    from concourse.bass_utils import run_bass_kernel_spmd

    f = lambda a: np.ascontiguousarray(a)
    W, b, C = (np.asarray(a) for a in (L1_gnn_W, L1_gnn_b, L1_gnn_C))
    w1 = np.zeros((FEAT, TILES, QUADS, PAD), W.dtype)
    w1[:, :, :, :HEAD] = W.transpose(1, 0, 2).reshape(FEAT, TILES, QUADS, HEAD)
    b1 = np.zeros((QUADS, PAD, TILES), b.dtype)
    b1[:, :HEAD, :] = b.reshape(TILES, QUADS, HEAD).transpose(1, 2, 0)
    c1 = np.zeros((QUADS, PAD, TILES, QUADS, PAD), C.dtype)
    for h in range(HEADS):
        t, q = h // QUADS, h % QUADS
        c1[q, :HEAD, t, q, :HEAD] = C[h].T
    arrays = {
        "x": f(x), "adj": f(adj), "mask": f(nodemask), "mask_t": f(np.asarray(nodemask).T),
        "w0": f(L0_gnn_W), "w1": f(w1.reshape(FEAT, TILES, 128)), "b1": f(b1.reshape(128, TILES)),
        "c1": f(c1.reshape(128, TILES, 128)),
        "w2t": f(np.asarray(L2_gnn_weight).transpose(2, 0, 1)),
        "wiht": f(np.asarray(L2_gnn_w_ih).T),
        "whht": f(np.asarray(L2_gnn_w_hh).T.reshape(FEAT, 3, FEAT)),
        "bih": f(np.asarray(L2_gnn_b_ih).reshape(3, FEAT).T),
        "bhh": f(np.asarray(L2_gnn_b_hh).reshape(3, FEAT).T),
        "w3": f(L3_gnn_weight), "b3": f(L3_gnn_bias),
    }
    nc = bacc.Bacc("TRN2", target_bir_lowering=False, num_devices=1)
    args = {k: nc.dram_tensor(f"in_{k}", a.shape, mybir.dt.from_np(a.dtype), kind="ExternalInput").ap()
            for k, a in arrays.items()}
    cap_dram = nc.dram_tensor("cap_dram", (GRAPHS, NODES), F32, kind="Internal").ap()
    out = nc.dram_tensor("out_0", (GRAPHS, NODES, FEAT), F32, kind="ExternalOutput").ap()
    build(nc, cap_dram=cap_dram, out=out, **args)
    r = run_bass_kernel_spmd(nc, [{f"in_{k}": a for k, a in arrays.items()}], core_ids=[0])
    return r.results[0]["out_0"]
```

```python
from contextlib import ExitStack

import concourse.bass as bass
from concourse import mybir

F32 = mybir.dt.float32
F32R = mybir.dt.float32r
I32 = mybir.dt.int32
ALU = mybir.AluOpType
ACT = mybir.ActivationFunctionType
X_AXIS = mybir.AxisListType.X

GRAPHS, NODES, FEAT = 128, 128, 128
GROUP = 4
SLOTS = 2
ROUNDS = GRAPHS // (GROUP * SLOTS)
LAG = 2
HALF = GROUP // 2
HEADS, HEAD = 8, 16
PAD = 32
QUADS = 4
TILES = HEADS // QUADS
PAIR = 2
LAYERS = 5
NORMS = 4
NEG = -1e30
TOP = 3e38
EPS = 1e-5


class Slot:

    def __init__(self, n, sb, psum, sem):
        self.n = n

        def tile(name, dt=F32):
            return sb(f"{name}{n}", [128, GROUP, 128], dt)

        def done(name):
            return sem(f"s_{name}{n}")

        self.XIN = tile("XIN")
        self.ADJ = tile("ADJ")
        self.CAP = tile("CAP")
        self.X1 = tile("X1")
        self.X2 = tile("X2")
        self.X3 = tile("X3")
        self.X3B = tile("X3B")
        self.OUT = tile("OUT")
        self.HA = tile("HA")
        self.HAT = tile("HAT")
        self.IT = tile("IT")
        self.A01 = tile("A01")
        self.ADJT = tile("ADJT")
        self.XT = sb(f"XT{n}", [128, TILES, GROUP, 128])
        self.YTH = sb(f"YTH{n}", [128, TILES, GROUP, PAIR, 128], F32R)
        self.YTL = sb(f"YTL{n}", [128, TILES, GROUP, PAIR, 128], F32R)
        self.XN = sb(f"XN{n}", [128, TILES, GROUP, 128])
        self.OT = sb(f"OT{n}", [128, TILES, GROUP, 128])
        self.SC = sb(f"SC{n}", [128, QUADS, HALF, PAIR, 128])
        self.XTS = sb(f"XTS{n}", [128, TILES, GROUP, 128], F32R)
        softmax = self.SC[:, :, :, :, :].rearrange("p q b c n -> p q (b c) n")
        self.ZRAW = softmax[:, 0]
        self.Z = softmax[:, 1]
        self.E = softmax[:, 2]
        self.ET = softmax[:, 3]
        self.R, self.ZG = self.XT[:, 0], self.XT[:, 1]
        self.OMZ, self.ZH = self.XN[:, 0], self.XN[:, 1]
        self.NG, self.Q = self.OT[:, 0], self.OT[:, 1]
        self.H = tile("H")
        self.HT = tile("HT")
        self.HTH = tile("HTH", F32R)
        self.HTL = tile("HTL", F32R)
        self.AGH = tile("AGH", F32R)
        self.AGL = tile("AGL", F32R)
        self.T = tile("T")
        self.CV = tile("CV")
        self.STAT = sb(f"STAT{n}", [128, NORMS, GROUP, 6])
        self.COUNT = sb(f"COUNT{n}", [128, NORMS, GROUP])
        self.MV = sb(f"MV{n}", [128, NORMS, GROUP, 2])
        self.NMEAN = sb(f"NMEAN{n}", [128, NORMS, GROUP])
        self.VE = sb(f"VE{n}", [128, NORMS, GROUP])
        self.RSTD = sb(f"RSTD{n}", [128, NORMS, GROUP])
        self.SHIFT = sb(f"SHIFT{n}", [128, NORMS, GROUP])
        self.NMAX = sb(f"NMAX{n}", [128, GROUP])
        self.SUM = sb(f"SUM{n}", [128, GROUP])
        self.RSUM = sb(f"RSUM{n}", [128, GROUP])
        self.P = [psum(f"P{n}_{b}", [128, GROUP, 128], F32) for b in range(4)]

        self.s_x_in = done("x_in")
        self.s_adj_in = done("adj_in")
        self.s_cap_in = done("cap_in")
        self.s_out_done = done("out_done")
        self.s_rows_x = done("rows_x")
        self.s_rows = done("rows")
        self.s_scale_x = done("scale_x")
        self.s_scale = done("scale")
        self.s_ha = done("ha")
        self.s_h = done("h")
        self.s_adjt_ps = done("adjt_ps")
        self.s_adjt = done("adjt")
        self.s_a01 = done("a01")
        self.s_hat_ps = done("hat_ps")
        self.s_hat = done("hat")
        self.s_it_ps = done("it_ps")
        self.s_it = done("it")
        self.s_sim_ps = done("sim_ps")
        self.s_z_raw = done("z_raw")
        self.s_z = done("z")
        self.s_nmax = done("nmax")
        self.s_e = done("e")
        self.s_rsum = done("rsum")
        self.s_et_ps = done("et_ps")
        self.s_et = done("et")
        self.s_att_ps = done("att_ps")
        self.s_x1 = done("x1")
        self.s_xt_ps = done("xt_ps")
        self.s_xt = done("xt")
        self.s_xh = done("xh")
        self.s_xs = done("xs")
        self.s_xn_ps = done("xn_ps")
        self.s_xn = done("xn")
        self.s_yt_ps = done("yt_ps")
        self.s_yt = done("yt")
        self.s_yl = done("yl")
        self.s_sc_ps = done("sc_ps")
        self.s_sc = done("sc")
        self.s_alpha = done("alpha")
        self.s_heads_ps = done("heads_ps")
        self.s_ot = done("ot")
        self.s_ott_ps = done("ott_ps")
        self.s_x2 = done("x2")
        self.s_h2t_ps = done("h2t_ps")
        self.s_ht = done("ht")
        self.s_hth = done("hth")
        self.s_htl = done("htl")
        self.s_agg_ps = done("agg_ps")
        self.s_agh = done("agh")
        self.s_agl = done("agl")
        self.s_n_ps = done("n_ps")
        self.s_r_ps = done("r_ps")
        self.s_z_ps = done("z_ps")
        self.s_in_ps = done("in_ps")
        self.s_r = done("r")
        self.s_zg = done("zg")
        self.s_omz = done("omz")
        self.s_zh = done("zh")
        self.s_t = done("t")
        self.s_u = done("u")
        self.s_ng = done("ng")
        self.s_q = done("q")
        self.s_hn_ps = done("hn_ps")
        self.s_hn = done("hn")
        self.s_x3 = done("x3")
        self.s_x3b = done("x3b")
        self.s_cv_ps = done("cv_ps")
        self.s_cv = done("cv")
        self.s_out_ps = done("out_ps")
        self.s_out = done("out")


def build(nc, x, adj, mask, mask_t, w0, w1, b1, c1, share, lower, w2t, wiht, whht, bih, bhh, w3, b3, cap_dram, out):
    ctx = ExitStack()
    with ctx:
        def sb(name, shape, dt=F32):
            return ctx.enter_context(nc.sbuf_tensor(name, shape, dt))

        def psum(name, shape, dt):
            return ctx.enter_context(nc.psum_tensor(name, shape, dt))

        def sem(name):
            return ctx.enter_context(nc.semaphore(name))

        W0 = sb("W0", [128, FEAT])
        W1 = sb("W1", [128, TILES, 128])
        B1 = sb("B1", [128, TILES])
        C1 = sb("C1", [128, TILES, 128])
        LOWER = sb("LOWER", [128, 1])
        SHARE = sb("SHARE", [128, PAIR])
        BIH = sb("BIH", [128, 3])
        BHH = sb("BHH", [128, 3])
        BRZ = sb("BRZ", [128, 3])
        VH = sb("VH", [128, LAYERS, 3, FEAT], F32R)
        VL = sb("VL", [128, LAYERS, 3, FEAT], F32R)
        WHHH = sb("WHHH", [128, 3, FEAT], F32R)
        WHHL = sb("WHHL", [128, 3, FEAT], F32R)
        W3 = sb("W3", [128, FEAT])
        B3 = sb("B3", [128, FEAT])
        MASKT = sb("MASKT", [128, GRAPHS])
        IDENT = sb("IDENT", [128, 128])
        MINUS_HALF = sb("MINUS_HALF", [128, GROUP])
        EPSILON = sb("EPSILON", [128, GROUP])
        ZEROS = sb("ZEROS", [128, GROUP])

        s_weights = sem("s_weights")
        s_masks = sem("s_masks")
        s_zero = sem("s_zero")
        s_ident = sem("s_ident")
        s_half = sem("s_half")
        s_mask01 = sem("s_mask01")
        s_caps = sem("s_caps")
        s_caps_out = sem("s_caps_out")
        s_maskt = sem("s_maskt")
        s_brz = sem("s_brz")
        s_v_ps = sem("s_v_ps")
        s_vh = sem("s_vh")
        s_vl = sem("s_vl")
        s_whhh = sem("s_whhh")
        s_whhl = sem("s_whhl")

        slots = [Slot(n, sb, psum, sem) for n in range(SLOTS)]
        first, second = slots

        ZERO = first.Q[:, 0, :]
        MASK = first.T[:, 0, :].bitcast(I32)
        MASK01 = first.T[:, 1, :]
        CAPS = first.T[:, 2, :]
        MASKT_I = first.T[:, 3, :].bitcast(I32)
        WIHT = first.SC[:, 0, :, :, :].rearrange("p a b n -> p (a b n)")[:, 0:3 * FEAT]
        WHHT = first.SC[:, 1, :, :, :].rearrange("p a b n -> p (a b) n")[:, 0:3, :]
        W2T = second.SC[:, 0:2, :, :, :].rearrange("p q a b n -> p (q a b) n")[:, 0:LAYERS, :]

        def after(eng, semaphore, n):
            if not isinstance(n, int) or n > 0:
                eng.wait_ge(semaphore, n)

        def at(stage, S, i, *part):
            if not isinstance(i, int) or 0 <= i < ROUNDS:
                stage(S, i, *part)

        def pipeline(eng, one_round):
            for n in range(LAG + 1):
                one_round(n)
            with eng.Fori(LAG + 1, ROUNDS - 1) as n:
                one_round(n)
            for n in range(ROUNDS - 1, ROUNDS + LAG):
                one_round(n)

        N_WEIGHTS = 16 * 13

        STAT_STEPS = 2 * GROUP + 1
        SCALE_STEPS = 4

        def norm_sems(S, i, norm):
            if norm == 0:
                return S.s_rows_x, S.s_scale_x, i
            return S.s_rows, S.s_scale, (NORMS - 1) * i + norm - 1

        block = ctx.enter_context(nc.Block())

        @block.sync
        def _(sp):
            def load_x(S, i):
                g = i * (SLOTS * GROUP) + S.n * GROUP
                after(sp, S.s_x1, i * GROUP)
                sp.dma_start(S.XIN[:, :, :],
                             x[bass.ds(g, GROUP), :, :].rearrange("b n d -> n b d"))\
                    .then_inc(S.s_x_in, 16)

            def load_adj(S, i):
                g = i * (SLOTS * GROUP) + S.n * GROUP
                after(sp, S.s_z_raw, 2 * i)
                after(sp, S.s_a01, i)
                after(sp, S.s_adjt_ps, i)
                sp.dma_start(S.ADJ[:, :, :],
                             adj[bass.ds(g, GROUP), :, :].rearrange("b n d -> n b d"))\
                    .then_inc(S.s_adj_in, 16)

            def load_cap(S, i):
                g = i * (SLOTS * GROUP) + S.n * GROUP
                after(sp, S.s_z, 2 * i)
                sp.dma_start(S.CAP[:, :, :],
                             cap_dram[bass.ds(g, GROUP), :].partition_broadcast(128))\
                    .then_inc(S.s_cap_in, 16)

            def load_next(load, S, i):
                if not isinstance(i, int) or i + 1 < ROUNDS:
                    load(S, i + 1)

            def next_x(S, i):
                load_next(load_x, S, i)

            def next_adj(S, i):
                load_next(load_adj, S, i)

            def next_cap(S, i):
                load_next(load_cap, S, i)

            def store(S, i):
                g = i * (SLOTS * GROUP) + S.n * GROUP
                sp.wait_ge(S.s_out, i + 1)
                sp.dma_start(out[bass.ds(g, GROUP), :, :].rearrange("b n d -> n b d"),
                             S.OUT[:, :, :]).then_inc(S.s_out_done, 16)

            sp.dma_start(MASK, mask).then_inc(s_masks, 16)
            sp.dma_start(MASKT_I, mask_t).then_inc(s_masks, 16)
            load_x(first, 0)
            load_x(second, 0)
            load_adj(first, 0)
            load_adj(second, 0)
            sp.wait_ge(s_caps, 1)
            sp.dma_start(cap_dram[:, :], CAPS).then_inc(s_caps_out, 16)
            sp.wait_ge(s_caps_out, 16)
            for S in slots:
                load_cap(S, 0)

            def one_round(n):
                at(next_cap, first, n)
                at(next_cap, second, n)
                at(next_x, first, n)
                at(store, first, n - 1)
                at(next_x, second, n)
                at(next_adj, first, n)
                at(store, second, n - 1)
                at(next_adj, second, n)

            pipeline(sp, one_round)
            for S in slots:
                sp.wait_ge(S.s_out_done, 16 * ROUNDS)

        @block.tensor
        def _(pe):
            pe.wait_ge(s_weights, N_WEIGHTS)
            for l in range(LAYERS):
                bank = (second.P + first.P[3:])[l].rearrange("p b n -> p (b n)")
                pe.matmul(bank[:, 0:3 * FEAT], W2T[:, l, :], WIHT, start=True, stop=True)\
                    .then_inc(s_v_ps, 1)
            pe.wait_ge(s_ident, 1)
            pe.wait_ge(s_vl, LAYERS)
            pe.wait_ge(s_whhl, 1)

            def turn(bank, src):
                for b in range(GROUP):
                    last = pe.transpose(bank[:, b, :], src[:, b, :], IDENT[:, :])
                return last


            def turn_ha(S, i, norm):
                pe.wait_ge(S.s_ha, GROUP * (2 * i + norm + 1))
                if norm == 0:
                    after(pe, S.s_zg, LAYERS * i - 1)
                turn(S.P[3], S.HA).then_inc(S.s_hat_ps, 1)

            def inter(S, i):
                pe.wait_ge(S.s_hat, 2 * i + 1)
                after(pe, S.s_r, LAYERS * i - 1)
                pe.matmul(S.P[2][:, :, :], W0[:, :], S.HAT[:, :, :], start=True, stop=True)\
                    .then_inc(S.s_it_ps, 1)

            def similarities(S, i):
                pe.wait_ge(S.s_it, i + 1)
                after(pe, S.s_zg, LAYERS * i)
                for b in range(GROUP):
                    last = pe.matmul(S.P[3][:, b, :], S.IT[:, b, :], S.HAT[:, b, :],
                                     start=True, stop=True)
                last.then_inc(S.s_sim_ps, 1)


            def keep_warm(S, i):
                pe.wait_ge(S.s_hat, 2 * i + 1)
                after(pe, S.s_x3, GROUP * i)
                pe.matmul(S.P[0][:, :, :], W0[:, :], S.HAT[:, :, :], start=True, stop=True)

            def keep_warm_late(S, i):
                pe.wait_ge(S.s_sc, 2 * QUADS * (i + 1))
                pe.matmul(S.P[3][:, :, :], W0[:, :], S.HAT[:, :, :], start=True, stop=True)

            def turn_e(S, i):
                pe.wait_ge(S.s_e, GROUP * (i + 1))
                turn(S.P[3], S.E).then_inc(S.s_et_ps, 1)

            def attend(S, i):
                pe.wait_ge(S.s_et, i + 1)
                after(pe, S.s_x3, GROUP * i)
                for b in range(GROUP):
                    last = pe.matmul(S.P[0][:, b, :], S.ET[:, b, :], S.HA[:, b, :],
                                     start=True, stop=True)
                last.then_inc(S.s_att_ps, 1)

            def turn_adj(S, i):
                pe.wait_ge(S.s_adj_in, 16 * (i + 1))
                after(pe, S.s_cv, i)
                turn(S.P[1], S.ADJ).then_inc(S.s_adjt_ps, 1)

            def head_features(S, i, t):
                if t == 0:
                    pe.wait_ge(S.s_hat, 2 * i + 2)
                    pe.wait_ge(S.s_adjt, i + 1)
                    after(pe, S.s_out, i)
                pe.matmul(S.P[1 + t][:, :, :], W1[:, t, :], S.HAT[:, :, :],
                          start=True, stop=True).then_inc(S.s_xt_ps, 1)

            def head_features_c(S, i, t):
                pe.wait_ge(S.s_xh, TILES * i + t + 1)
                pe.matmul(S.P[1 + t][:, :, :], C1[:, t, :], S.XT[:, t, :, :],
                          start=True, stop=True).then_inc(S.s_yt_ps, 1)

            def turn_head_features(S, i):
                pe.wait_ge(S.s_xt, TILES * (i + 1))
                for t, bank in ((0, S.P[0]), (1, S.P[3])):
                    for b in range(GROUP):
                        last = pe.transpose(bank[:, b, :], S.XT[:, t, b, :], IDENT[:, :])
                    last.then_inc(S.s_xn_ps, 1)

            def scores(S, i, k, t):
                if k == 0:
                    pe.wait_ge(S.s_yl, TILES * PAIR * i + PAIR * (t + 1))
                    pe.wait_ge(S.s_xs, TILES * i + t + 1)
                    pe.wait_ge(S.s_xn, TILES * i + t + 1)
                else:
                    pe.wait_ge(S.s_sc, QUADS * 2 * i + PAIR * (t + 1))
                    if t == 1:
                        pe.wait_ge(S.s_ot, 2 * i + 1)
                for b in range(HALF):
                    for y, start in ((S.YTH, True), (S.YTL, False)):
                        for r in range(PAIR):
                            rows = slice(PAD * PAIR * r, PAD * PAIR * (r + 1))
                            last = pe.matmul(S.P[PAIR * t + r][:, PAIR * b:PAIR * b + PAIR, :],
                                             S.XTS[rows, t, HALF * k + b, :],
                                             y[rows, t, HALF * k + b, :, :],
                                             start=start, stop=not start)
                last.then_inc(S.s_sc_ps, 1)

            def heads(S, i, k):
                bank = S.P[0 if k else 3]
                pe.wait_ge(S.s_alpha, QUADS * (2 * i + k + 1))
                for b in range(HALF):
                    for t in range(TILES):
                        for q in range(QUADS):
                            rows = slice(PAD * q, PAD * q + PAD)
                            last = pe.matmul(bank[rows, HALF * t + b, :],
                                             S.XN[:, t, HALF * k + b, rows],
                                             S.SC[:, PAIR * t + q // PAIR, b, q % PAIR, :],
                                             start=True, stop=True)
                last.then_inc(S.s_heads_ps, 1)

            def turn_heads(S, i, k):
                pe.wait_ge(S.s_ot, 2 * i + k + 1)
                if k == 0:
                    pe.wait_ge(S.s_sc, QUADS * (2 * i + 2))
                for b in range(HALF):
                    for t in range(TILES):
                        last = pe.transpose(S.P[1 + k][:, TILES * b + t, :],
                                            S.OT[:, t, HALF * k + b, :], IDENT[:, :])
                last.then_inc(S.s_ott_ps, 1)


            def turn_h2(S, i):
                pe.wait_ge(S.s_h, GROUP * (2 * i + 1))
                turn(S.P[0], S.H).then_inc(S.s_h2t_ps, 1)

            def hidden(bank, c, S):
                pe.matmul(bank[:, :, :], WHHH[:, c, :], S.HTH[:, :, :], start=True, stop=False)
                pe.matmul(bank[:, :, :], WHHL[:, c, :], S.HTH[:, :, :], start=False, stop=False)

            def gates_hidden(S, i, l):
                if l == LAYERS - 1 and (not isinstance(i, int) or i + 1 < ROUNDS):
                    pe.wait_ge(S.s_hat, 2 * i + 3)
                    pe.wait_ge(S.s_it, i + 2)
                pe.wait_ge(S.s_hth, LAYERS * i + l + 1)
                hidden(S.P[2], 0, S)
                hidden(S.P[3], 1, S)

            def aggregate(S, i, l):
                if l == 0:
                    pe.wait_ge(S.s_a01, i + 1)
                    pe.wait_ge(S.s_ht, (LAYERS + 1) * i + 1)
                else:
                    pe.wait_ge(S.s_hn, (LAYERS - 1) * i + l)
                for b in range(GROUP):
                    last = pe.matmul(S.P[0][:, b, :], S.H[:, b, :], S.A01[:, b, :],
                                     start=True, stop=True)
                last.then_inc(S.s_agg_ps, 1)

            def gates_low(S, i, l):
                hidden(S.P[1], 2, S)
                pe.wait_ge(S.s_htl, LAYERS * i + l + 1)
                pe.matmul(S.P[1][:, :, :], WHHH[:, 2, :], S.HTL[:, :, :], start=False, stop=True)\
                    .then_inc(S.s_n_ps, 1)
                pe.matmul(S.P[2][:, :, :], WHHH[:, 0, :], S.HTL[:, :, :], start=False, stop=False)
                pe.matmul(S.P[3][:, :, :], WHHH[:, 1, :], S.HTL[:, :, :], start=False, stop=False)

            def gates_input(S, i, l):
                pe.wait_ge(S.s_agh, LAYERS * i + l + 1)
                for c in (0, 1):
                    bank = S.P[2 + c]
                    pe.matmul(bank[:, :, :], VH[:, l, c, :], S.AGH[:, :, :], start=False, stop=False)
                    pe.matmul(bank[:, :, :], VL[:, l, c, :], S.AGH[:, :, :], start=False, stop=False)
                pe.wait_ge(S.s_agl, LAYERS * i + l + 1)
                pe.matmul(S.P[2][:, :, :], VH[:, l, 0, :], S.AGL[:, :, :], start=False, stop=True)\
                    .then_inc(S.s_r_ps, 1)
                pe.matmul(S.P[3][:, :, :], VH[:, l, 1, :], S.AGL[:, :, :], start=False, stop=True)\
                    .then_inc(S.s_z_ps, 1)
                pe.matmul(S.P[0][:, :, :], VH[:, l, 2, :], S.AGH[:, :, :], start=True, stop=False)
                pe.matmul(S.P[0][:, :, :], VL[:, l, 2, :], S.AGH[:, :, :], start=False, stop=False)
                pe.matmul(S.P[0][:, :, :], VH[:, l, 2, :], S.AGL[:, :, :], start=False, stop=True)\
                    .then_inc(S.s_in_ps, 1)

            def turn_new(S, i, l):
                pe.wait_ge(S.s_ht, (LAYERS + 1) * i + l + 2)
                turn(S.P[0], S.HT).then_inc(S.s_hn_ps, 1)


            def conv(S, i):
                pe.wait_ge(S.s_h, GROUP * (2 * i + 2))
                for b in range(GROUP):
                    last = pe.matmul(S.P[1][:, b, :], S.H[:, b, :], S.ADJT[:, b, :],
                                     start=True, stop=True)
                last.then_inc(S.s_cv_ps, 1)

            def conv_out(S, i):
                pe.wait_ge(S.s_cv, i + 1)
                for b in range(GROUP):
                    last = pe.matmul(S.P[2][:, b, :], S.CV[:, b, :], W3[:, :],
                                     start=True, stop=True)
                last.then_inc(S.s_out_ps, 1)

            def one_round(n):
                at(scores, second, n - 1, 0, 0)
                at(scores, second, n - 1, 0, 1)
                at(heads, first, n - 1, 0)
                at(scores, first, n - 1, 1, 0)
                at(scores, first, n - 1, 1, 1)
                at(heads, second, n - 1, 0)
                at(scores, second, n - 1, 1, 0)
                at(scores, second, n - 1, 1, 1)
                at(heads, first, n - 1, 1)
                at(turn_heads, first, n - 1, 0)
                at(turn_heads, first, n - 1, 1)
                at(heads, second, n - 1, 1)
                at(turn_heads, second, n - 1, 0)
                at(keep_warm_late, first, n - 1)
                at(turn_heads, second, n - 1, 1)
                at(keep_warm_late, second, n - 1)
                at(keep_warm_late, first, n - 1)
                at(turn_h2, first, n - 1)
                at(keep_warm_late, second, n - 1)
                at(gates_hidden, first, n - 1, 0)
                at(aggregate, first, n - 1, 0)
                at(gates_low, first, n - 1, 0)
                at(turn_h2, second, n - 1)
                at(gates_input, first, n - 1, 0)
                at(aggregate, second, n - 1, 0)
                at(gates_hidden, second, n - 1, 0)
                at(gates_low, second, n - 1, 0)
                at(gates_input, second, n - 1, 0)
                at(turn_new, first, n - 1, 0)
                at(gates_hidden, first, n - 1, 1)
                at(aggregate, first, n - 1, 1)
                at(gates_low, first, n - 1, 1)
                at(gates_input, first, n - 1, 1)
                at(turn_new, second, n - 1, 0)
                at(gates_hidden, second, n - 1, 1)
                at(aggregate, second, n - 1, 1)
                at(gates_low, second, n - 1, 1)
                at(gates_input, second, n - 1, 1)
                at(turn_new, first, n - 1, 1)
                at(gates_hidden, first, n - 1, 2)
                at(aggregate, first, n - 1, 2)
                at(gates_low, first, n - 1, 2)
                at(gates_input, first, n - 1, 2)
                at(turn_new, second, n - 1, 1)
                at(gates_hidden, second, n - 1, 2)
                at(aggregate, second, n - 1, 2)
                at(gates_low, second, n - 1, 2)
                at(gates_input, second, n - 1, 2)
                at(turn_new, first, n - 1, 2)
                at(gates_hidden, first, n - 1, 3)
                at(aggregate, first, n - 1, 3)
                at(gates_low, first, n - 1, 3)
                at(gates_input, first, n - 1, 3)
                at(turn_new, second, n - 1, 2)
                at(gates_hidden, second, n - 1, 3)
                at(turn_ha, first, n, 0)
                at(aggregate, second, n - 1, 3)
                at(gates_low, second, n - 1, 3)
                at(inter, first, n)
                at(turn_new, first, n - 1, 3)
                at(gates_input, second, n - 1, 3)
                at(gates_hidden, first, n - 1, 4)
                at(aggregate, first, n - 1, 4)
                at(gates_low, first, n - 1, 4)
                at(turn_ha, second, n, 0)
                at(gates_input, first, n - 1, 4)
                at(inter, second, n)
                at(turn_new, second, n - 1, 3)
                at(similarities, first, n)
                at(gates_hidden, second, n - 1, 4)
                at(aggregate, second, n - 1, 4)
                at(gates_low, second, n - 1, 4)
                at(turn_new, first, n - 1, 4)
                at(gates_input, second, n - 1, 4)
                at(keep_warm, first, n)
                at(similarities, second, n)
                at(keep_warm, first, n)
                at(turn_e, first, n)
                at(attend, first, n)
                at(conv, first, n - 1)
                at(turn_new, second, n - 1, 4)
                at(conv_out, first, n - 1)
                at(turn_adj, first, n)
                at(turn_e, second, n)
                at(keep_warm, second, n)
                at(keep_warm, second, n)
                at(turn_ha, first, n, 1)
                at(attend, second, n)
                at(head_features, first, n, 0)
                at(head_features, first, n, 1)
                at(head_features_c, first, n, 0)
                at(conv, second, n - 1)
                at(head_features_c, first, n, 1)
                at(turn_head_features, first, n)
                at(turn_adj, second, n)
                at(conv_out, second, n - 1)
                at(turn_ha, second, n, 1)
                at(scores, first, n, 0, 0)
                at(head_features, second, n, 0)
                at(head_features, second, n, 1)
                at(head_features_c, second, n, 0)
                at(scores, first, n, 0, 1)
                at(head_features_c, second, n, 1)
                at(turn_head_features, second, n)

            pipeline(pe, one_round)

        @block.scalar
        def _(act):
            for dst, src in [(W2T, w2t), (WIHT, wiht), (WHHT, whht), (W0[:, :], w0),
                             (BIH[:, :], bih), (BHH[:, :], bhh), (W1[:, :, :], w1), (B1[:, :], b1),
                             (C1[:, :, :], c1), (SHARE[:, :], share), (LOWER[:, :], lower), (W3[:, :], w3),
                             (B3[:, :], b3.partition_broadcast(128))]:
                act.dma_start(dst, src).then_inc(s_weights, 16)
            act.wait_ge(s_weights, N_WEIGHTS)
            act.wait_ge(s_brz, 1)

            def normed(S, i, norm, k):
                src = (S.XIN, S.X1, S.X2, S.X3)[norm]
                dst, done = ((S.HA, S.s_ha), (S.HA, S.s_ha), (S.H, S.s_h), (S.H, S.s_h))[norm]
                if k == 0:
                    scaled, before = norm_sems(S, i, norm)[1:]
                    act.wait_ge(scaled, SCALE_STEPS * (before + 1))
                    if norm == 0:
                        after(act, S.s_att_ps, i)
                        after(act, S.s_hat_ps, 2 * i)
                    elif norm == 2:
                        after(act, S.s_cv_ps, i)
                for b in range(HALF * k, HALF * k + HALF):
                    act.activation(dst[:, b, :], src[:, b, :], ACT.Relu,
                                   bias=S.SHIFT[:, norm, b:b + 1], scale=S.RSTD[:, norm, b:b + 1])\
                        .then_inc(done, 1)

            def adj_t(S, i):
                act.wait_ge(S.s_adjt_ps, i + 1)
                act.copy(S.ADJT[:, :, :], S.P[1][:, :, :]).then_inc(S.s_adjt, 1)

            def ha_t(S, i, norm):
                act.wait_ge(S.s_hat_ps, 2 * i + norm + 1)
                act.copy(S.HAT[:, :, :], S.P[3][:, :, :]).then_inc(S.s_hat, 1)

            def exps(S, i, k):
                act.wait_ge(S.s_nmax, 2 * i + k + 1)
                for b in range(HALF * k, HALF * k + HALF):
                    act.activation(S.E[:, b, :], S.Z[:, b, :], ACT.Exp,
                                   bias=S.NMAX[:, b:b + 1], accum_out=S.SUM[:, b:b + 1])\
                        .then_inc(S.s_e, 1)

            def e_t(S, i):
                act.wait_ge(S.s_et_ps, i + 1)
                act.copy(S.ET[:, :, :], S.P[3][:, :, :]).then_inc(S.s_et, 1)

            def features(S, i, t):
                act.wait_ge(S.s_xt_ps, TILES * i + t + 1)
                act.activation(S.XT[:, t, :, :], S.P[1 + t][:, :, :], ACT.Identity,
                               bias=B1[:, t:t + 1]).then_inc(S.s_xt, 1)
                act.activation(S.XTS[:, t, :, :], S.P[1 + t][:, :, :], ACT.Identity,
                               bias=B1[:, t:t + 1]).then_inc(S.s_xh, 1)

            def features_c(S, i, t):
                act.wait_ge(S.s_yt_ps, TILES * i + t + 1)
                for p in range(PAIR):
                    act.activation(S.YTH[:, t, :, p, :], S.P[1 + t][:, :, :], ACT.Identity,
                                   scale=SHARE[:, p:p + 1]).then_inc(S.s_yt, 1)

            def features_natural(S, i):
                for t, bank in ((0, S.P[0]), (1, S.P[3])):
                    act.wait_ge(S.s_xn_ps, TILES * i + t + 1)
                    act.copy(S.XN[:, t, :, :], bank[:, :, :]).then_inc(S.s_xn, 1)

            def alphas(S, i, k, q):
                act.wait_ge(S.s_sc, QUADS * (2 * i + k) + q + 1)
                act.activation(S.SC[:, q, :, :, :], S.SC[:, q, :, :, :], ACT.Tanh)\
                    .then_inc(S.s_alpha, 1)

            def h_t(S, i):
                act.wait_ge(S.s_h2t_ps, i + 1)
                act.copy(S.HTH[:, :, :], S.P[0][:, :, :]).then_inc(S.s_hth, 1)
                act.copy(S.HT[:, :, :], S.P[0][:, :, :]).then_inc(S.s_ht, 1)

            def aggregated(S, i, l):
                act.wait_ge(S.s_agg_ps, LAYERS * i + l + 1)
                act.copy(S.AGH[:, :, :], S.P[0][:, :, :]).then_inc(S.s_agh, 1)

            def gates(S, i, l):
                act.wait_ge(S.s_r_ps, LAYERS * i + l + 1)
                act.activation(S.R[:, :, :], S.P[2][:, :, :], ACT.Sigmoid, bias=BRZ[:, 0:1])\
                    .then_inc(S.s_r, 1)
                act.wait_ge(S.s_z_ps, LAYERS * i + l + 1)
                act.activation(S.ZG[:, :, :], S.P[3][:, :, :], ACT.Sigmoid, bias=BRZ[:, 1:2])\
                    .then_inc(S.s_zg, 1)

            def gate_n(S, i, l):
                act.wait_ge(S.s_u, LAYERS * i + l + 1)
                act.activation(S.NG[:, :, :], S.T[:, :, :], ACT.Tanh, bias=BIH[:, 2:3])\
                    .then_inc(S.s_ng, 1)

            def h_natural(S, i, l):
                act.wait_ge(S.s_hn_ps, LAYERS * i + l + 1)
                act.copy(S.H[:, :, :], S.P[0][:, :, :]).then_inc(S.s_hn, 1)

            def conved(S, i):
                act.wait_ge(S.s_cv_ps, i + 1)
                act.copy(S.CV[:, :, :], S.P[1][:, :, :]).then_inc(S.s_cv, 1)

            def one_round(n):
                at(features_c, first, n - 1, 0)
                at(normed, second, n - 1, 1, 0)
                at(conved, second, n - 2)
                at(normed, second, n - 1, 1, 1)
                at(features_natural, first, n - 1)
                at(adj_t, second, n - 1)
                at(ha_t, second, n - 1, 1)
                at(features_c, first, n - 1, 1)
                at(features, second, n - 1, 0)
                at(features, second, n - 1, 1)
                at(features_c, second, n - 1, 0)
                at(features_c, second, n - 1, 1)
                at(features_natural, second, n - 1)
                at(alphas, first, n - 1, 0, 0)
                at(alphas, first, n - 1, 0, 1)
                at(alphas, first, n - 1, 0, 2)
                at(alphas, first, n - 1, 0, 3)
                at(alphas, second, n - 1, 0, 0)
                at(alphas, second, n - 1, 0, 2)
                at(alphas, second, n - 1, 0, 3)
                at(alphas, second, n - 1, 0, 1)
                at(alphas, first, n - 1, 1, 1)
                at(alphas, first, n - 1, 1, 0)
                at(alphas, first, n - 1, 1, 3)
                at(alphas, first, n - 1, 1, 2)
                at(alphas, second, n - 1, 1, 1)
                at(alphas, second, n - 1, 1, 2)
                at(alphas, second, n - 1, 1, 0)
                at(alphas, second, n - 1, 1, 3)
                at(normed, first, n - 1, 2, 0)
                at(normed, first, n - 1, 2, 1)
                at(h_t, first, n - 1)
                at(normed, second, n - 1, 2, 0)
                at(normed, second, n - 1, 2, 1)
                at(aggregated, first, n - 1, 0)
                at(normed, first, n, 0, 0)
                at(h_t, second, n - 1)
                at(gates, first, n - 1, 0)
                at(aggregated, second, n - 1, 0)
                at(normed, first, n, 0, 1)
                at(gate_n, first, n - 1, 0)
                at(gates, second, n - 1, 0)
                at(h_natural, first, n - 1, 0)
                at(aggregated, first, n - 1, 1)
                at(gate_n, second, n - 1, 0)
                at(gates, first, n - 1, 1)
                at(h_natural, second, n - 1, 0)
                at(aggregated, second, n - 1, 1)
                at(gate_n, first, n - 1, 1)
                at(gates, second, n - 1, 1)
                at(h_natural, first, n - 1, 1)
                at(gate_n, second, n - 1, 1)
                at(aggregated, first, n - 1, 2)
                at(gates, first, n - 1, 2)
                at(h_natural, second, n - 1, 1)
                at(normed, second, n, 0, 0)
                at(aggregated, second, n - 1, 2)
                at(gate_n, first, n - 1, 2)
                at(gates, second, n - 1, 2)
                at(h_natural, first, n - 1, 2)
                at(gate_n, second, n - 1, 2)
                at(aggregated, first, n - 1, 3)
                at(normed, second, n, 0, 1)
                at(gates, first, n - 1, 3)
                at(h_natural, second, n - 1, 2)
                at(gate_n, first, n - 1, 3)
                at(ha_t, first, n, 0)
                at(aggregated, second, n - 1, 3)
                at(h_natural, first, n - 1, 3)
                at(gates, second, n - 1, 3)
                at(gate_n, second, n - 1, 3)
                at(aggregated, first, n - 1, 4)
                at(ha_t, second, n, 0)
                at(gates, first, n - 1, 4)
                at(h_natural, second, n - 1, 3)
                at(gate_n, first, n - 1, 4)
                at(aggregated, second, n - 1, 4)
                at(gates, second, n - 1, 4)
                at(exps, first, n, 0)
                at(exps, first, n, 1)
                at(gate_n, second, n - 1, 4)
                at(e_t, first, n)
                at(normed, first, n - 1, 3, 0)
                at(normed, first, n - 1, 3, 1)
                at(exps, second, n, 0)
                at(conved, first, n - 1)
                at(exps, second, n, 1)
                at(adj_t, first, n)
                at(normed, first, n, 1, 0)
                at(normed, first, n, 1, 1)
                at(e_t, second, n)
                at(ha_t, first, n, 1)
                at(normed, second, n - 1, 3, 0)
                at(features, first, n, 0)
                at(normed, second, n - 1, 3, 1)
                at(features, first, n, 1)

            pipeline(act, one_round)

        @block.gpsimd
        def _(pool):
            pool.memset(ZERO, 0.0).then_inc(s_zero, 1)
            pool.memset(MINUS_HALF[:, :], -0.5).then_inc(s_half, 1)
            pool.memset(EPSILON[:, :], EPS).then_inc(s_half, 1)
            pool.memset(ZEROS[:, :], 0.0).then_inc(s_half, 1)
            pool.wait_ge(s_zero, 1)
            pool.affine_select(out=IDENT[:, :], in_=ZERO, compare_op=ALU.not_equal, fill=1.0,
                               base=0, pattern=[[-1, 128]], channel_multiplier=1)\
                .then_inc(s_ident, 1)
            pool.wait_ge(s_half, 3)
            pool.wait_ge(s_weights, N_WEIGHTS)
            pool.wait_ge(s_ident, 1)

            def scales(S, i, norm):
                rows, scaled, before = norm_sems(S, i, norm)
                pool.wait_ge(rows, STAT_STEPS * (before + 1))
                pool.tensor_tensor(S.VE[:, norm, :], S.MV[:, norm, :, 1], EPSILON[:, :], ALU.add)\
                    .then_inc(scaled, 1)
                pool.tensor_tensor(S.NMEAN[:, norm, :], ZEROS[:, :], S.MV[:, norm, :, 0],
                                   ALU.subtract).then_inc(scaled, 1)
                pool.wait_ge(scaled, SCALE_STEPS * before + 2)
                pool.tensor_tensor(S.RSTD[:, norm, :], S.VE[:, norm, :], MINUS_HALF[:, :], ALU.pow)\
                    .then_inc(scaled, 1)
                pool.wait_ge(scaled, SCALE_STEPS * before + 3)
                pool.tensor_tensor(S.SHIFT[:, norm, :], S.NMEAN[:, norm, :], S.RSTD[:, norm, :],
                                   ALU.mult).then_inc(scaled, 1)

            def h_low(S, i, l):
                pool.wait_ge(S.s_ht, (LAYERS + 1) * i + l + 1)
                pool.wait_ge(S.s_hth, LAYERS * i + l + 1)
                pool.tensor_tensor(S.HTL[:, :, :], S.HT[:, :, :], S.HTH[:, :, :].bitcast(F32),
                                   ALU.subtract).then_inc(S.s_htl, 1)

            def mix(S, i, l):
                pool.wait_ge(S.s_zg, LAYERS * i + l + 1)
                pool.tensor_tensor(S.ZH[:, :, :], S.ZG[:, :, :], S.HT[:, :, :], ALU.mult)\
                    .then_inc(S.s_zh, 1)

            def bias_out(S, i):
                pool.wait_ge(S.s_x3, GROUP * (i + 1))
                pool.tensor_tensor(S.X3B[:, :, :], S.X3[:, :, :],
                                   B3[:, :].unsqueeze(1).to_broadcast([128, GROUP, FEAT]),
                                   ALU.add).then_inc(S.s_x3b, 1)

            def one_round(n):
                at(scales, second, n - 2, 3)
                at(scales, second, n - 1, 1)
                at(bias_out, second, n - 2)
                at(scales, first, n - 1, 2)
                at(scales, first, n, 0)
                at(scales, second, n - 1, 2)
                at(h_low, first, n - 1, 0)
                at(h_low, second, n - 1, 0)
                at(mix, first, n - 1, 0)
                at(h_low, first, n - 1, 1)
                at(mix, second, n - 1, 0)
                at(h_low, second, n - 1, 1)
                at(mix, first, n - 1, 1)
                at(h_low, first, n - 1, 2)
                at(mix, second, n - 1, 1)
                at(scales, second, n, 0)
                at(h_low, second, n - 1, 2)
                at(mix, first, n - 1, 2)
                at(h_low, first, n - 1, 3)
                at(mix, second, n - 1, 2)
                at(h_low, second, n - 1, 3)
                at(mix, first, n - 1, 3)
                at(h_low, first, n - 1, 4)
                at(mix, second, n - 1, 3)
                at(h_low, second, n - 1, 4)
                at(mix, first, n - 1, 4)
                at(mix, second, n - 1, 4)
                at(scales, first, n - 1, 3)
                at(scales, first, n, 1)
                at(bias_out, first, n - 1)

            pipeline(pool, one_round)

        @block.vector
        def _(dve):
            dve.wait_ge(s_masks, 32)
            dve.tensor_scalar(MASK01, MASK, 0.0, None, ALU.not_equal).then_inc(s_mask01, 1)
            dve.tensor_copy(MASKT[:, :], MASKT_I).then_inc(s_maskt, 1)
            dve.wait_ge(s_mask01, 1)
            dve.tensor_scalar(CAPS, MASK01, TOP, NEG, ALU.mult, ALU.add).then_inc(s_caps, 1)
            dve.wait_ge(s_weights, N_WEIGHTS)
            dve.tensor_tensor(BRZ[:, :], BIH[:, :], BHH[:, :], ALU.add).then_inc(s_brz, 1)
            dve.tensor_copy(WHHH[:, :, :], WHHT).then_inc(s_whhh, 1)
            dve.wait_ge(s_whhh, 1)
            dve.tensor_tensor(WHHL[:, :, :], WHHT, WHHH[:, :, :].bitcast(F32), ALU.subtract)\
                .then_inc(s_whhl, 1)
            for l in range(LAYERS):
                dve.wait_ge(s_v_ps, l + 1)
                bank = (second.P + first.P[3:])[l]
                dve.tensor_copy(VH[:, l, :, :], bank[:, 0:3, :]).then_inc(s_vh, 1)
                dve.wait_ge(s_vh, l + 1)
                dve.tensor_tensor(VL[:, l, :, :], bank[:, 0:3, :], VH[:, l, :, :].bitcast(F32),
                                  ALU.subtract).then_inc(s_vl, 1)
            dve.wait_ge(s_maskt, 1)
            dve.wait_ge(s_whhl, 1)

            def stats(S, i, norm, k):
                src = (S.XIN, S.X1, S.X2, S.X3)[norm]
                rows = norm_sems(S, i, norm)[0]
                if norm == 0:
                    dve.wait_ge(S.s_x_in, 16 * (i + 1))
                elif norm == 1:
                    dve.wait_ge(S.s_x1, GROUP * (i + 1))
                elif norm == 2:
                    dve.wait_ge(S.s_x2, 2 * (i + 1))
                else:
                    dve.wait_ge(S.s_x3, GROUP * (i + 1))
                for b in range(HALF * k, HALF * k + HALF):
                    dve.bn_stats(S.STAT[:, norm, b, :], src[:, b, :]).then_inc(rows, 1)

            def means(S, i, norm):
                rows, _, before = norm_sems(S, i, norm)
                dve.wait_ge(rows, STAT_STEPS * before + GROUP)
                dve.tensor_copy(S.COUNT[:, norm, :], S.STAT[:, norm, :, 0]).then_inc(rows, 1)
                for b in range(GROUP):
                    dve.bn_aggr(S.MV[:, norm, b, :], S.STAT[:, norm, b, :]).then_inc(rows, 1)

            def adj_nonzero(S, i):
                dve.wait_ge(S.s_adj_in, 16 * (i + 1))
                dve.tensor_scalar(S.A01[:, :, :], S.ADJ[:, :, :], 0.0, None, ALU.not_equal)\
                    .then_inc(S.s_a01, 1)

            def inter(S, i):
                dve.wait_ge(S.s_it_ps, i + 1)
                dve.tensor_copy(S.IT[:, :, :], S.P[2][:, :, :]).then_inc(S.s_it, 1)

            def times_adj(S, i, k):
                if k == 0:
                    dve.wait_ge(S.s_sim_ps, i + 1)
                    dve.wait_ge(S.s_adj_in, 16 * (i + 1))
                two = slice(HALF * k, HALF * k + HALF)
                dve.tensor_tensor(S.ZRAW[:, two, :], S.P[3][:, two, :], S.ADJ[:, two, :], ALU.mult)\
                    .then_inc(S.s_z_raw, 1)

            def capped(S, i, k):
                dve.wait_ge(S.s_z_raw, 2 * i + k + 1)
                dve.wait_ge(S.s_cap_in, 16 * (i + 1))
                two = slice(HALF * k, HALF * k + HALF)
                dve.tensor_tensor(S.Z[:, two, :], S.ZRAW[:, two, :], S.CAP[:, two, :], ALU.min)\
                    .then_inc(S.s_z, 1)

            def maxima(S, i, k):
                dve.wait_ge(S.s_z, 2 * i + k + 1)
                two = slice(HALF * k, HALF * k + HALF)
                dve.tensor_reduce(S.NMAX[:, two], S.Z[:, two, :], X_AXIS, ALU.max, negate=True)\
                    .then_inc(S.s_nmax, 1)

            def add_attention(S, i):
                dve.wait_ge(S.s_e, GROUP * (i + 1))
                dve.reciprocal(S.RSUM[:, :], S.SUM[:, :]).then_inc(S.s_rsum, 1)
                dve.wait_ge(S.s_rsum, i + 1)
                dve.wait_ge(S.s_att_ps, i + 1)
                for b in range(GROUP):
                    dve.scalar_tensor_tensor(out=S.X1[:, b, :], in0=S.P[0][:, b, :],
                                             scalar=S.RSUM[:, b:b + 1], in1=S.XIN[:, b, :],
                                             op0=ALU.mult, op1=ALU.add).then_inc(S.s_x1, 1)

            def weigh_scores(S, i, k, q):
                dve.wait_ge(S.s_sc_ps, TILES * (2 * i + k) + q // PAIR + 1)
                if k == 1 and q == 0:
                    dve.wait_ge(S.s_heads_ps, 2 * i + 1)
                both = S.ADJT[:, HALF * k:HALF * k + HALF, :].unsqueeze(2)\
                    .to_broadcast([128, HALF, PAIR, 128])
                bank = S.P[q][:, :, :].rearrange("p (b c) n -> p b c n", c=PAIR)
                dve.tensor_tensor(S.SC[:, q, :, :, :], bank, both, ALU.mult).then_inc(S.s_sc, 1)

            def features_split(S, i, t):
                dve.wait_ge(S.s_xh, TILES * i + t + 1)
                dve.wait_ge(S.s_xt, TILES * i + t + 1)
                dve.scalar_tensor_tensor(out=S.XTS[:, t, :, :],
                                         in0=S.XTS[:, t, :, :].bitcast(F32),
                                         scalar=LOWER[:, 0:1], in1=S.XT[:, t, :, :],
                                         op0=ALU.mult, op1=ALU.add).then_inc(S.s_xs, 1)

            def features_c_low(S, i, t):
                dve.wait_ge(S.s_yt, TILES * PAIR * i + PAIR * (t + 1))
                for p in range(PAIR):
                    dve.scalar_tensor_tensor(out=S.YTL[:, t, :, p, :], in0=S.P[1 + t][:, :, :],
                                             scalar=SHARE[:, p:p + 1],
                                             in1=S.YTH[:, t, :, p, :].bitcast(F32),
                                             op0=ALU.mult, op1=ALU.subtract).then_inc(S.s_yl, 1)

            def heads_out(S, i, k):
                dve.wait_ge(S.s_heads_ps, 2 * i + k + 1)
                bank = S.P[0 if k else 3][:, :, :].rearrange("p (t b) n -> p t b n", b=HALF)
                dve.tensor_copy(S.OT[:, :, HALF * k:HALF * k + HALF, :], bank)\
                    .then_inc(S.s_ot, 1)

            def add_heads(S, i, k):
                dve.wait_ge(S.s_ott_ps, 2 * i + k + 1)
                graphs = slice(HALF * k, HALF * k + HALF)
                real = S.P[1 + k][:, :, :].rearrange("p (b t) (q w) -> p b (t q) w",
                                                     t=TILES, w=PAD)[:, :, :, 0:HEAD]
                dve.tensor_tensor(
                    S.X2[:, graphs, :].rearrange("p b (h w) -> p b h w", w=HEAD), real,
                    S.X1[:, graphs, :].rearrange("p b (h w) -> p b h w", w=HEAD), ALU.add)\
                    .then_inc(S.s_x2, 1)

            def aggregate_low(S, i, l):
                dve.wait_ge(S.s_agh, LAYERS * i + l + 1)
                dve.tensor_tensor(S.AGL[:, :, :], S.P[0][:, :, :], S.AGH[:, :, :].bitcast(F32),
                                  ALU.subtract).then_inc(S.s_agl, 1)

            def reset(S, i, l):
                if S is first and isinstance(i, int) and i == 0 and l == 0:
                    dve.wait_ge(s_caps_out, 16)
                dve.wait_ge(S.s_n_ps, LAYERS * i + l + 1)
                dve.wait_ge(S.s_r, LAYERS * i + l + 1)
                dve.scalar_tensor_tensor(out=S.T[:, :, :], in0=S.P[1][:, :, :],
                                         scalar=BHH[:, 2:3], in1=S.R[:, :, :],
                                         op0=ALU.add, op1=ALU.mult).then_inc(S.s_t, 1)

            def one_minus_z(S, i, l):
                dve.wait_ge(S.s_zg, LAYERS * i + l + 1)
                dve.tensor_scalar(S.OMZ[:, :, :], S.ZG[:, :, :], -1.0, 1.0, ALU.mult, ALU.add)\
                    .then_inc(S.s_omz, 1)

            def n_input(S, i, l):
                dve.wait_ge(S.s_t, LAYERS * i + l + 1)
                dve.wait_ge(S.s_in_ps, LAYERS * i + l + 1)
                dve.tensor_tensor(S.T[:, :, :], S.P[0][:, :, :], S.T[:, :, :], ALU.add)\
                    .then_inc(S.s_u, 1)

            def n_share(S, i, l):
                dve.wait_ge(S.s_omz, LAYERS * i + l + 1)
                dve.wait_ge(S.s_ng, LAYERS * i + l + 1)
                dve.tensor_tensor(S.Q[:, :, :], S.NG[:, :, :], S.OMZ[:, :, :], ALU.mult)\
                    .then_inc(S.s_q, 1)

            def new_high(S, i, l):
                dve.wait_ge(S.s_zh, LAYERS * i + l + 1)
                dve.wait_ge(S.s_q, LAYERS * i + l + 1)
                dve.tensor_tensor(S.HTH[:, :, :], S.Q[:, :, :], S.ZH[:, :, :], ALU.add)\
                    .then_inc(S.s_hth, 1)

            def new(S, i, l):
                dve.wait_ge(S.s_zh, LAYERS * i + l + 1)
                dve.wait_ge(S.s_q, LAYERS * i + l + 1)
                dve.tensor_tensor(S.HT[:, :, :], S.Q[:, :, :], S.ZH[:, :, :], ALU.add)\
                    .then_inc(S.s_ht, 1)

            def add_hidden(S, i):
                dve.wait_ge(S.s_hn_ps, LAYERS * (i + 1))
                for b in range(GROUP):
                    graph = i * (SLOTS * GROUP) + S.n * GROUP + b
                    dve.scalar_tensor_tensor(out=S.X3[:, b, :], in0=S.P[0][:, b, :],
                                             scalar=MASKT[:, bass.ds(graph, 1)],
                                             in1=S.X2[:, b, :],
                                             op0=ALU.mult, op1=ALU.add).then_inc(S.s_x3, 1)

            def result(S, i):
                dve.wait_ge(S.s_out_ps, i + 1)
                dve.wait_ge(S.s_x3b, i + 1)
                after(dve, S.s_out_done, 16 * i)
                dve.tensor_tensor(S.OUT[:, :, :], S.P[2][:, :, :], S.X3B[:, :, :], ALU.add)\
                    .then_inc(S.s_out, 1)

            def one_round(n):
                at(stats, first, n, 0, 0)
                at(features_c_low, first, n - 1, 0)
                at(stats, first, n, 0, 1)
                at(features_split, first, n - 1, 1)
                at(means, first, n, 0)
                at(result, second, n - 2)
                at(weigh_scores, first, n - 1, 0, 0)
                at(features_c_low, first, n - 1, 1)
                at(weigh_scores, first, n - 1, 0, 1)
                at(features_split, second, n - 1, 0)
                at(features_split, second, n - 1, 1)
                at(weigh_scores, first, n - 1, 0, 2)
                at(features_c_low, second, n - 1, 0)
                at(features_c_low, second, n - 1, 1)
                at(weigh_scores, first, n - 1, 0, 3)
                at(weigh_scores, second, n - 1, 0, 0)
                at(weigh_scores, second, n - 1, 0, 1)
                at(weigh_scores, second, n - 1, 0, 2)
                at(weigh_scores, second, n - 1, 0, 3)
                at(heads_out, first, n - 1, 0)
                at(weigh_scores, first, n - 1, 1, 0)
                at(weigh_scores, first, n - 1, 1, 1)
                at(weigh_scores, first, n - 1, 1, 2)
                at(weigh_scores, first, n - 1, 1, 3)
                at(heads_out, second, n - 1, 0)
                at(weigh_scores, second, n - 1, 1, 0)
                at(weigh_scores, second, n - 1, 1, 1)
                at(weigh_scores, second, n - 1, 1, 2)
                at(heads_out, first, n - 1, 1)
                at(weigh_scores, second, n - 1, 1, 3)
                at(add_heads, first, n - 1, 0)
                at(add_heads, first, n - 1, 1)
                at(stats, first, n - 1, 2, 0)
                at(stats, first, n - 1, 2, 1)
                at(means, first, n - 1, 2)
                at(heads_out, second, n - 1, 1)
                at(add_heads, second, n - 1, 1)
                at(add_heads, second, n - 1, 0)
                at(stats, second, n - 1, 2, 0)
                at(stats, second, n - 1, 2, 1)
                at(means, second, n - 1, 2)
                at(stats, second, n, 0, 0)
                at(aggregate_low, first, n - 1, 0)
                at(adj_nonzero, second, n - 1)
                at(reset, first, n - 1, 0)
                at(n_input, first, n - 1, 0)
                at(one_minus_z, first, n - 1, 0)
                at(aggregate_low, second, n - 1, 0)
                at(n_share, first, n - 1, 0)
                at(new, first, n - 1, 0)
                at(new_high, first, n - 1, 0)
                at(reset, second, n - 1, 0)
                at(stats, second, n, 0, 1)
                at(n_input, second, n - 1, 0)
                at(one_minus_z, second, n - 1, 0)
                at(aggregate_low, first, n - 1, 1)
                at(n_share, second, n - 1, 0)
                at(new, second, n - 1, 0)
                at(new_high, second, n - 1, 0)
                at(means, second, n, 0)
                at(reset, first, n - 1, 1)
                at(one_minus_z, first, n - 1, 1)
                at(n_input, first, n - 1, 1)
                at(aggregate_low, second, n - 1, 1)
                at(n_share, first, n - 1, 1)
                at(new, first, n - 1, 1)
                at(new_high, first, n - 1, 1)
                at(reset, second, n - 1, 1)
                at(n_input, second, n - 1, 1)
                at(one_minus_z, second, n - 1, 1)
                at(n_share, second, n - 1, 1)
                at(aggregate_low, first, n - 1, 2)
                at(new_high, second, n - 1, 1)
                at(new, second, n - 1, 1)
                at(one_minus_z, first, n - 1, 2)
                at(reset, first, n - 1, 2)
                at(n_input, first, n - 1, 2)
                at(aggregate_low, second, n - 1, 2)
                at(n_share, first, n - 1, 2)
                at(new, first, n - 1, 2)
                at(new_high, first, n - 1, 2)
                at(reset, second, n - 1, 2)
                at(n_input, second, n - 1, 2)
                at(one_minus_z, second, n - 1, 2)
                at(n_share, second, n - 1, 2)
                at(aggregate_low, first, n - 1, 3)
                at(new_high, second, n - 1, 2)
                at(new, second, n - 1, 2)
                at(reset, first, n - 1, 3)
                at(n_input, first, n - 1, 3)
                at(one_minus_z, first, n - 1, 3)
                at(n_share, first, n - 1, 3)
                at(new, first, n - 1, 3)
                at(aggregate_low, second, n - 1, 3)
                at(inter, first, n)
                at(new_high, first, n - 1, 3)
                at(reset, second, n - 1, 3)
                at(n_input, second, n - 1, 3)
                at(one_minus_z, second, n - 1, 3)
                at(n_share, second, n - 1, 3)
                at(aggregate_low, first, n - 1, 4)
                at(new, second, n - 1, 3)
                at(new_high, second, n - 1, 3)
                at(reset, first, n - 1, 4)
                at(one_minus_z, first, n - 1, 4)
                at(inter, second, n)
                at(n_input, first, n - 1, 4)
                at(times_adj, first, n, 0)
                at(capped, first, n, 0)
                at(n_share, first, n - 1, 4)
                at(new, first, n - 1, 4)
                at(times_adj, first, n, 1)
                at(aggregate_low, second, n - 1, 4)
                at(maxima, first, n, 0)
                at(capped, first, n, 1)
                at(add_hidden, first, n - 1)
                at(maxima, first, n, 1)
                at(stats, first, n - 1, 3, 0)
                at(reset, second, n - 1, 4)
                at(stats, first, n - 1, 3, 1)
                at(n_input, second, n - 1, 4)
                at(times_adj, second, n, 0)
                at(means, first, n - 1, 3)
                at(capped, second, n, 0)
                at(one_minus_z, second, n - 1, 4)
                at(times_adj, second, n, 1)
                at(n_share, second, n - 1, 4)
                at(capped, second, n, 1)
                at(new, second, n - 1, 4)
                at(maxima, second, n, 0)
                at(add_attention, first, n)
                at(stats, first, n, 1, 0)
                at(stats, first, n, 1, 1)
                at(means, first, n, 1)
                at(maxima, second, n, 1)
                at(add_hidden, second, n - 1)
                at(stats, second, n - 1, 3, 0)
                at(stats, second, n - 1, 3, 1)
                at(means, second, n - 1, 3)
                at(result, first, n - 1)
                at(add_attention, second, n)
                at(stats, second, n, 1, 0)
                at(stats, second, n, 1, 1)
                at(means, second, n, 1)
                at(adj_nonzero, first, n)
                at(features_split, first, n, 0)

            pipeline(dve, one_round)


def kernel(x, adj, nodemask, L0_gnn_W, L1_gnn_W, L1_gnn_b, L1_gnn_C, L2_gnn_weight, L2_gnn_w_ih,
           L2_gnn_w_hh, L2_gnn_b_ih, L2_gnn_b_hh, L3_gnn_weight, L3_gnn_bias):
    import numpy as np
    import concourse.bacc as bacc
    from concourse.bass_utils import run_bass_kernel_spmd

    f = lambda a: np.ascontiguousarray(a)
    W, b, C = (np.asarray(a) for a in (L1_gnn_W, L1_gnn_b, L1_gnn_C))
    w1 = np.zeros((FEAT, TILES, QUADS, PAD), W.dtype)
    w1[:, :, :, :HEAD] = W.transpose(1, 0, 2).reshape(FEAT, TILES, QUADS, HEAD)
    w1[:, :, :, HEAD:] = w1[:, :, :, :HEAD]
    b1 = np.zeros((QUADS, PAD, TILES), b.dtype)
    b1[:, :HEAD, :] = b.reshape(TILES, QUADS, HEAD).transpose(1, 2, 0)
    b1[:, HEAD:, :] = b1[:, :HEAD, :]
    c1 = np.zeros((QUADS, PAD, TILES, QUADS, PAD), C.dtype)
    for h in range(HEADS):
        t, q = h // QUADS, h % QUADS
        c1[q, :HEAD, t, q, :HEAD] = C[h].T
        c1[q, :HEAD, t, q, HEAD:] = C[h].T
    share = np.arange(128)[:, None] // PAD % PAIR == np.arange(PAIR)
    arrays = {
        "x": f(x), "adj": f(adj), "mask": f(nodemask), "mask_t": f(np.asarray(nodemask).T),
        "w0": f(L0_gnn_W), "w1": f(w1.reshape(FEAT, TILES, 128)), "b1": f(b1.reshape(128, TILES)),
        "c1": f(c1.reshape(128, TILES, 128)),
        "lower": f(-(np.arange(128)[:, None] % PAD >= HEAD).astype(C.dtype)),
        "share": f(share.astype(C.dtype)),
        "w2t": f(np.asarray(L2_gnn_weight).transpose(2, 0, 1)),
        "wiht": f(np.asarray(L2_gnn_w_ih).T),
        "whht": f(np.asarray(L2_gnn_w_hh).T.reshape(FEAT, 3, FEAT)),
        "bih": f(np.asarray(L2_gnn_b_ih).reshape(3, FEAT).T),
        "bhh": f(np.asarray(L2_gnn_b_hh).reshape(3, FEAT).T),
        "w3": f(L3_gnn_weight), "b3": f(L3_gnn_bias),
    }
    nc = bacc.Bacc("TRN2", target_bir_lowering=False, num_devices=1)
    args = {k: nc.dram_tensor(f"in_{k}", a.shape, mybir.dt.from_np(a.dtype), kind="ExternalInput").ap()
            for k, a in arrays.items()}
    cap_dram = nc.dram_tensor("cap_dram", (GRAPHS, NODES), F32, kind="Internal").ap()
    out = nc.dram_tensor("out_0", (GRAPHS, NODES, FEAT), F32, kind="ExternalOutput").ap()
    build(nc, cap_dram=cap_dram, out=out, **args)
    r = run_bass_kernel_spmd(nc, [{f"in_{k}": a for k, a in arrays.items()}], core_ids=[0])
    return r.results[0]["out_0"]
```
